# Optimizing a Trainium2 kernel written in Bass

```python
import numpy as np
import jax
import jax.numpy as jnp

def _softmax(x, axis=-1):
    return jax.nn.softmax(x, axis=axis)

def _gelu(x):
    return jax.nn.gelu(x, approximate=True)

def _silu(x):
    return jax.nn.silu(x)

def _sigmoid(x):
    return jax.nn.sigmoid(x)

def _layernorm(x, axis=-1, eps=1e-05):
    m = jnp.mean(x, axis=axis, keepdims=True)
    v = jnp.var(x, axis=axis, keepdims=True)
    return (x - m) / jnp.sqrt(v + eps)

def _scatter_add(tgt, idx, src, axis=0):
    return tgt.at[idx].add(src)

def _segment_sum(src, seg, n):
    return jax.ops.segment_sum(src, seg, n)
kernel_name = 'mk_xattn_ffn_d1_seqx_r4_301bf4'

def setup_inputs(seed: int=0):
    np.random.seed(seed)
    _w = jnp.asarray

    def _rec_inputs():
        import jax
        import jax.numpy as jnp
        _rk = jax.random.key(seed)
        x = 7.22e-05 + 1 * jax.random.normal(jax.random.fold_in(_rk, 1), (4, 512, 512), jnp.float32)
        _lenS = 512 - jax.random.randint(jax.random.fold_in(_rk, 7), (4,), 0, max(1, 512 // 4) + 1, jnp.int32)
        _lenS2 = 512 - jax.random.randint(jax.random.fold_in(_rk, 8), (4,), 0, max(1, 512 // 4) + 1, jnp.int32)
        _ctx_1024P = jax.random.normal(jax.random.fold_in(_rk, 11), (4, 16, 256), jnp.float32)
        _ctx_1024c = jax.random.dirichlet(jax.random.fold_in(_rk, 511), 0.3 * jnp.ones((16,), jnp.float32), (4, 512))
        _ctx_1024t = jnp.einsum('bsk,bkd->bsd', _ctx_1024c, _ctx_1024P)
        _ctx_1024t = _ctx_1024t * jax.lax.rsqrt(jnp.mean(jnp.square(_ctx_1024t)) + 1e-12) * 0.953939
        ctx_1024 = 2.81802e-05 + 1.00001 * (_ctx_1024t + 0.3 * jax.random.normal(jax.random.fold_in(_rk, 611), (4, 512, 256), jnp.float32))
        return (x, ctx_1024)
    x, ctx_1024 = _rec_inputs()

    def _L0_xattn_setup():
        import jax, jax.numpy as jnp
        import numpy as np
        key = jax.random.key(seed)
        ks = jax.random.split(key, 6)
        B, L, N, C, D = (8, 128, 512, 256, 128)
        return {'teacher_logits': jax.random.normal(ks[0], (B, L, N), dtype=jnp.float32), 'teacher_features': jax.random.normal(ks[1], (B, N, C), dtype=jnp.float32), 'Wq': jax.random.normal(ks[2], (D, C), dtype=jnp.float32) * (1.0 / np.sqrt(C)), 'bq': jnp.zeros((D,), dtype=jnp.float32), 'Wk': jax.random.normal(ks[3], (D, C), dtype=jnp.float32) * (1.0 / np.sqrt(C)), 'bk': jnp.zeros((D,), dtype=jnp.float32)}
    _L0_xattn_all = _L0_xattn_setup()
    _L0_xattn_in = {k: v for k, v in _L0_xattn_all.items() if k in ('Wq', 'bq', 'Wk', 'bk')}
    del _L0_xattn_all

    def _L0_ffn_setup():
        import jax, jax.numpy as jnp
        import numpy as np
        B, S, H, I = (1, 64, 512, 1536)

        def _quantized_matmul(x, w, scale):
            wq = w.astype(jnp.float8_e4m3fn).astype(x.dtype)
            y = jnp.einsum('bsi,io->bso', x, wq)
            return y * scale
        key = jax.random.key(seed)
        ks = jax.random.split(key, 7)
        return {'x': jax.random.normal(ks[0], (B, S, H), dtype=jnp.float32), 'gate_w': jax.random.normal(ks[1], (H, I), dtype=jnp.float32) * 0.02, 'up_w': jax.random.normal(ks[2], (H, I), dtype=jnp.float32) * 0.02, 'down_w': jax.random.normal(ks[3], (I, H), dtype=jnp.float32) * 0.02, 'gate_scale': jax.random.uniform(ks[4], (I,), dtype=jnp.float32, minval=0.5, maxval=1.5), 'up_scale': jax.random.uniform(ks[5], (I,), dtype=jnp.float32, minval=0.5, maxval=1.5), 'down_scale': jax.random.uniform(ks[6], (H,), dtype=jnp.float32, minval=0.5, maxval=1.5)}
    _L0_ffn_all = _L0_ffn_setup()
    _L0_ffn_in = {k: v for k, v in _L0_ffn_all.items() if k in ('gate_w', 'up_w', 'down_w', 'gate_scale', 'up_scale', 'down_scale')}
    del _L0_ffn_all
    return {'x': x, 'ctx_1024': ctx_1024, 'L0_xattn_Wq': _L0_xattn_in['Wq'], 'L0_xattn_bq': _L0_xattn_in['bq'], 'L0_xattn_Wk': _L0_xattn_in['Wk'], 'L0_xattn_bk': _L0_xattn_in['bk'], 'L0_ffn_gate_w': _L0_ffn_in['gate_w'], 'L0_ffn_up_w': _L0_ffn_in['up_w'], 'L0_ffn_down_w': _L0_ffn_in['down_w'], 'L0_ffn_gate_scale': _L0_ffn_in['gate_scale'], 'L0_ffn_up_scale': _L0_ffn_in['up_scale'], 'L0_ffn_down_scale': _L0_ffn_in['down_scale']}

def reference(x, ctx_1024, L0_xattn_Wq, L0_xattn_bq, L0_xattn_Wk, L0_xattn_bk, L0_ffn_gate_w, L0_ffn_up_w, L0_ffn_down_w, L0_ffn_gate_scale, L0_ffn_up_scale, L0_ffn_down_scale):
    import jax
    import jax.numpy as jnp

    def _L0_xattn_ref(teacher_logits, teacher_features, Wq, bq, Wk, bk):
        import jax, jax.numpy as jnp
        import numpy as np
        query = jnp.einsum('bnc,dc->bnd', teacher_features, Wq) + bq
        key = jnp.einsum('bnc,dc->bnd', teacher_features, Wk) + bk
        energy = jnp.einsum('bnd,bmd->bnm', query, key)
        attention = jax.nn.softmax(energy, axis=-1)
        x_m = jnp.einsum('bln,bmn->blm', teacher_logits, attention)
        return x_m

    def _L0_ffn_ref(x, gate_w, up_w, down_w, gate_scale, up_scale, down_scale):
        import jax, jax.numpy as jnp
        import numpy as np
        B, S, H, I = (1, 64, 512, 1536)

        def _quantized_matmul(x, w, scale):
            wq = w.astype(jnp.float8_e4m3fn).astype(x.dtype)
            y = jnp.einsum('bsi,io->bso', x, wq)
            return y * scale
        gate = jax.nn.silu(_quantized_matmul(x, gate_w, gate_scale))
        up = _quantized_matmul(x, up_w, up_scale)
        fuse = gate * up
        return _quantized_matmul(fuse, down_w, down_scale)
    x = x + _L0_xattn_ref(_layernorm(x, axis=-1), ctx_1024, L0_xattn_Wq, L0_xattn_bq, L0_xattn_Wk, L0_xattn_bk)
    x = x + _L0_ffn_ref(_layernorm(x, axis=-1), L0_ffn_gate_w, L0_ffn_up_w, L0_ffn_down_w, L0_ffn_gate_scale, L0_ffn_up_scale, L0_ffn_down_scale)
    return x

_drawn_inputs = setup_inputs


def setup_inputs(seed=0):
    import zlib

    import numpy as np

    out = dict(_drawn_inputs(seed))
    spreads = {'L0_xattn_bq': (0.0, 0.1), 'L0_xattn_bk': (0.0, 0.1)}
    factors = {}
    for name, (base, spread) in spreads.items():
        noise = np.random.default_rng([zlib.crc32(name.encode()), seed]).standard_normal(out[name].shape)
        drawn = base * np.exp(spread * noise) if base else spread * noise
        out[name] = jnp.asarray(drawn.astype(out[name].dtype))
    for name, factor in factors.items():
        out[name] = (out[name] * factor).astype(out[name].dtype)
    return out
```

```python
from contextlib import ExitStack

import concourse.bass as bass
from concourse import mybir

F32 = mybir.dt.float32
F32R = mybir.dt.float32r
F16 = mybir.dt.float16
BF16 = mybir.dt.bfloat16
I32 = mybir.dt.int32
ALU = mybir.AluOpType
ACT = mybir.ActivationFunctionType
AX_X = mybir.AxisListType.X

P = 128
LN_EPS = 1e-5
H_SCALE = 2.0 ** 11
W_SHIFT = 2.0 ** -20
EXPONENT_BITS = 0x7F800000
HALF_BIT = 0x00400000
FLOOR = 1.5 * 2.0 ** -6


def build_xattn_ffn(nc, x, ctx_tokens, wq, bq, wk, bk, gate_w, up_w, down_w,
                    gate_scale, up_scale, down_scale, out):
    NB, L, H = x.shape
    N, C = ctx_tokens.shape[1:]
    D = wq.shape[0]
    I = gate_w.shape[1]
    LT, KT, NT, CT, IT = L // P, H // P, N // P, C // P, I // P
    NJ = IT // 2
    PRE = 1
    assert D == P and N == H and L == 512 and H == 512 and LT == KT == NT == 4 and CT == 2
    assert IT % 2 == 0 and PRE + NB - 1 <= NJ

    x_rows = x.rearrange("b (l p) h -> b p l h", p=P)
    out_rows = out.rearrange("b (l p) h -> b p l h", p=P)
    ctx_rows = ctx_tokens.rearrange("b (n p) c -> b p n c", p=P)
    gate_cols = gate_w.rearrange("(k p) (j c) -> j p k c", p=P, c=2 * P)
    up_cols = up_w.rearrange("(k p) (j c) -> j p k c", p=P, c=2 * P)
    down_rows = down_w.rearrange("(j t p) h -> j p t h", p=P, t=2)

    with ExitStack() as stack:
        def sb(name, shape, dt):
            return stack.enter_context(nc.sbuf_tensor(name, shape, dt))

        def sem(name):
            return stack.enter_context(nc.semaphore(name))

        x_all = sb("x_all", [P, NB * LT, H], F32)
        ctx_in = sb("ctx_in", [P, NT, C], F32)
        w_in = sb("w_in", [P, 2, C], F32)
        wT = sb("wT", [P, 2 * CT, D], F32)
        bias = sb("bias", [P, 2], F32)
        ident = sb("ident", [P, P], F32)
        norm = sb("norm", [P, LT, H], F32)
        xT = sb("xT", [P, KT, L], F32)
        ctxT = sb("ctxT", [P, CT, N], F32)
        qT = sb("qT", [P, N], F32)
        kT = sb("kT", [P, N], F32)
        attn = sb("attn", [P, NT, H], F32)
        attnT = sb("attnT", [P, NT, H], F32)
        part = sb("part", [P, 2 * LT, 6], F32)
        meanvar = sb("meanvar", [P, 2 * LT, 2], F32)
        ln_var = sb("ln_var", [P, 2, LT], F32)
        ln_mean = sb("ln_mean", [P, 2, LT], F32)
        ln_scale = sb("ln_scale", [P, 2 * NB, LT], F32)
        ln_shift = sb("ln_shift", [P, 2 * NB, LT], F32)
        minus_half = sb("minus_half", [P, LT], F32)
        neg_max = sb("neg_max", [P, NB * NT], F32)
        exp_sum = sb("exp_sum", [P, NB * NT], F32)
        inv_sum = sb("inv_sum", [P, NB * NT], F32)
        raw = sb("raw", [P, 3, 1024], F32)
        magic = sb("magic", [P, 3, 1024], F32)
        gate_q = sb("gate_q", [P, NJ, KT, 2 * P], BF16)
        up_q = sb("up_q", [P, NJ, KT, 2 * P], BF16)
        down_q = sb("down_q", [P, NJ, 2, H], F32R)
        scales_in = sb("scales_in", [2 * IT, P], F32)
        scales = sb("scales", [P, 2 * IT], F32)
        down_s = sb("down_s", [P, H], F32)
        hT_hi = sb("hT_hi", [P, KT, L], F16)
        hT_lo = sb("hT_lo", [P, KT, L], F16)
        silu = sb("silu", [P, 2, L], F32)
        fused = sb("fused", [P, 2, L], F32)
        f_hi = sb("f_hi", [P, 2, L], F32R)
        f_lo = sb("f_lo", [P, 2, L], F32R)
        y = sb("y", [P, LT, H], F32)

        bank = [stack.enter_context(nc.psum_tensor(f"bank{i}", [P, 512], F32)) for i in range(8)]
        t_bank, m_bank, e_bank, c_bank = bank[0:2], bank[2:4], bank[4:6], bank[6:8]
        acc_bank = bank[0:4]
        gu_bank = [bank[4:6], bank[6:8]]

        small_landed = sem("small_landed")
        down_s_landed = sem("down_s_landed")
        x_landed = [sem(f"x_landed{b}") for b in range(NB)]
        ctx_landed = [sem(f"ctx_landed{b}") for b in range(NB)]
        raw_landed = [sem(f"raw_landed{m}") for m in range(3)]
        x_here = sem("x_here")
        ctx_here = sem("ctx_here")
        consts_step = sem("consts_step")
        consts_done = sem("consts_done")
        down_s_done = sem("down_s_done")
        wT_filled, wT_done = sem("wT_filled"), sem("wT_done")
        scalesT_filled = sem("scalesT_filled")
        x_part, x_stats = sem("x_part"), sem("x_stats")
        h_part, h_stats = sem("h_part"), sem("h_stats")
        moments = [sem("x_moments"), sem("h_moments")]
        ln_step = [sem("x_ln_step"), sem("h_ln_step")]
        ln_done = [sem("x_ln_done"), sem("h_ln_done")]
        norm_done = sem("norm_done")
        normT_filled = sem("normT_filled")
        xT_even, xT_odd = sem("xT_even"), sem("xT_odd")
        ctxT_filled, ctxT_done = sem("ctxT_filled"), sem("ctxT_done")
        qk_filled, qk_done = sem("qk_filled"), sem("qk_done")
        energy_filled = sem("energy_filled")
        max_done, exp_done = sem("max_done"), sem("exp_done")
        inv_done, attn_done = sem("inv_done"), sem("attn_done")
        attnT_filled = sem("attnT_filled")
        attnT_even, attnT_odd = sem("attnT_even"), sem("attnT_odd")
        mixed = sem("mixed")
        x1_done = sem("x1_done")
        magic_done, shifted, summed = sem("magic_done"), sem("shifted"), sem("summed")
        weights_done = sem("weights_done")
        hT_hi_done, hT_lo_done = sem("hT_hi_done"), sem("hT_lo_done")
        gate_filled, up_filled = sem("gate_filled"), sem("up_filled")
        silu_done, fused_done = sem("silu_done"), sem("fused_done")
        f_hi_done, f_lo_done = sem("f_hi_done"), sem("f_lo_done")
        down_done = sem("down_done")
        y_done, out_done = sem("y_done"), sem("out_done")
        out_landed = sem("out_landed")

        def row(buf, i):
            return buf[:, bass.ds(i, 1), :].rearrange("p a n -> p (a n)")

        def col(buf, i):
            return buf[:, bass.ds(i, 1)]

        block = stack.enter_context(nc.Block())

        @block.sync
        def _(sp):
            raw_dst = [raw[:, 0, :].rearrange("p (k c) -> p k c", k=KT),
                       raw[:, 1, :].rearrange("p (k c) -> p k c", k=KT),
                       raw[:, 2, :].rearrange("p (t h) -> p t h", t=2)]
            raw_src = [gate_cols, up_cols, down_rows]

            def load_weights(j):
                for m in range(3):
                    dst = raw_dst[m]
                    sp.dma_start(dst, raw_src[m][bass.ds(j, 1)].rearrange("a p k c -> (a p) k c")
                                 ).then_inc(raw_landed[m], 16)

            sp.dma_start(ctx_in[:], ctx_rows[0]).then_inc(ctx_landed[0], 16)
            sp.dma_start(w_in[:, 0, :], wq).then_inc(small_landed, 16)
            sp.dma_start(w_in[:, 1, :], wk).then_inc(small_landed, 16)
            sp.dma_start(bias[:, 0:1], bq.rearrange("(p a) -> p a", a=1)).then_inc(small_landed, 16)
            sp.dma_start(bias[:, 1:2], bk.rearrange("(p a) -> p a", a=1)).then_inc(small_landed, 16)
            sp.dma_start(scales_in[0:IT, :], gate_scale.rearrange("(i p) -> i p", p=P)).then_inc(small_landed, 16)
            sp.dma_start(scales_in[IT:2 * IT, :], up_scale.rearrange("(i p) -> i p", p=P)
                         ).then_inc(small_landed, 16)
            sp.dma_start(x_all[:, 0:LT, :], x_rows[0]).then_inc(x_landed[0], 16)
            load_weights(0)
            sp.dma_start(down_s[:], down_scale.rearrange("(a h) -> a h", a=1).broadcast_to([P, H])
                         ).then_inc(down_s_landed, 16)
            for b in range(1, NB):
                sp.dma_start(x_all[:, b * LT:(b + 1) * LT, :], x_rows[b]).then_inc(x_landed[b], 16)
            sp.wait_ge(ctx_landed[0], 16)
            sp.sem_inc(ctx_here, 1)
            sp.wait_ge(x_landed[0], 16)
            sp.sem_inc(x_here, 1)
            for b in range(1, NB):
                sp.wait_ge(ctxT_filled, CT * b)
                sp.dma_start(ctx_in[:], ctx_rows[b]).then_inc(ctx_landed[b], 16)
                sp.wait_ge(ctx_landed[b], 16)
                sp.sem_inc(ctx_here, 1)
                sp.wait_ge(x_landed[b], 16)
                sp.sem_inc(x_here, 1)
                sp.wait_ge(weights_done, 3 * b)
                load_weights(b)
            with sp.Fori(NB, NJ) as j:
                sp.wait_ge(weights_done, j * 3)
                load_weights(j)
            with sp.Fori(0, NB) as b:
                for l in range(LT):
                    sp.wait_ge(out_done, b * LT + (l + 1))
                    sp.dma_start(out_rows[bass.ds(b, 1), :, l, :].rearrange("a p h -> (a p) h"), y[:, l, :]
                                 ).then_inc(out_landed, 16)
            sp.wait_ge(out_landed, 16 * NB * LT)

        @block.gpsimd
        def _(pool):
            nc.gpsimd.memset(ident[:], 0.0).then_inc(consts_step, 1)
            pool.wait_ge(consts_step, 1)
            nc.gpsimd.affine_select(out=ident[:], in_=ident[:], compare_op=ALU.not_equal, fill=1.0, base=0,
                                    pattern=[[-1, P]], channel_multiplier=1).then_inc(consts_done, 1)
            nc.gpsimd.memset(minus_half[:], -0.5).then_inc(consts_done, 1)
            pool.wait_ge(consts_done, 2)
            pool.sem_inc(ln_done[1], 1)

            def ln_factors(b, kind):
                s = b + kind * NB
                pool.wait_ge(moments[kind], b * 2 + 2)
                nc.gpsimd.tensor_tensor(row(ln_scale, s), ln_var[:, kind, :], minus_half[:], ALU.pow
                                        ).then_inc(ln_step[kind], 1)
                pool.wait_ge(ln_step[kind], b + 1)
                nc.gpsimd.tensor_tensor(row(ln_shift, s), ln_mean[:, kind, :], row(ln_scale, s), ALU.mult
                                        ).then_inc(ln_done[kind], 1)

            ln_factors(0, 0)
            with pool.Fori(0, NB - 1) as b:
                ln_factors(b + 1, 0)
                ln_factors(b, 1)
            ln_factors(NB - 1, 1)

            def add_residual(b):
                for l in range(LT):
                    pool.wait_ge(y_done, b * LT + (l + 1))
                    nc.gpsimd.tensor_tensor(y[:, l, :], y[:, l, :], row(x_all, b * LT + l), ALU.add
                                            ).then_inc(out_done, 1)

            with pool.Fori(0, NB) as b:
                add_residual(b)

        @block.vector
        def _(dve):
            def x_parts(b):
                for l in range(LT):
                    nc.vector.bn_stats(part[:, l, :], row(x_all, b * LT + l)).then_inc(x_part, 1)

            def h_parts(b, l):
                nc.vector.bn_stats(part[:, LT + l, :], row(x_all, b * LT + l)).then_inc(h_part, 1)

            def statistics(b, kind):
                stats = [x_stats, h_stats][kind]
                for l in range(LT):
                    nc.vector.bn_aggr(meanvar[:, kind * LT + l, :], part[:, kind * LT + l, :]).then_inc(stats, 1)
                if kind or not isinstance(b, int) or b:
                    dve.wait_ge(ln_done[kind], b + kind)
                dve.wait_ge(stats, b * LT + LT)
                mv = meanvar[:, kind * LT:(kind + 1) * LT, :]
                nc.vector.tensor_scalar(ln_var[:, kind, :], mv[:, :, 1], LN_EPS, H_SCALE ** -2, ALU.add, ALU.mult
                                        ).then_inc(moments[kind], 1)
                nc.vector.tensor_scalar_mul(ln_mean[:, kind, :], mv[:, :, 0], -1.0).then_inc(moments[kind], 1)

            def magic_numbers(j):
                for m in range(3):
                    dve.wait_ge(raw_landed[m], (j + 1) * 16)
                    nc.vector.tensor_scalar(magic[:, m, :].bitcast(I32), raw[:, m, :].bitcast(I32),
                                            EXPONENT_BITS, HALF_BIT, ALU.bitwise_and, ALU.bitwise_or
                                            ).then_inc(magic_done, 1)

            def round_sum(j, m):
                dve.wait_ge(shifted, j * 3 + (m + 1))
                nc.vector.scalar_tensor_tensor(raw[:, m, :], magic[:, m, :], FLOOR, raw[:, m, :],
                                               ALU.max, ALU.add).then_inc(summed, 1)

            def round_rest(j, m):
                dst = [gate_q, up_q, down_q][m][:, bass.ds(j, 1), :, :].rearrange("p a k c -> p (a k c)")
                dve.wait_ge(summed, j * 3 + (m + 1))
                nc.vector.scalar_tensor_tensor(dst, magic[:, m, :], FLOOR, raw[:, m, :],
                                               ALU.max, ALU.subtract).then_inc(weights_done, 1)

            def round_weights(j, m):
                round_sum(j, m)
                round_rest(j, m)

            def copy_xT(b, k):
                dve.wait_ge(normT_filled, b * KT + (k + 1))
                nc.vector.tensor_copy(xT[:, k, :], t_bank[k % 2][:]).then_inc(xT_odd, 1)

            def copy_attnT(b, k):
                dve.wait_ge(attnT_filled, b * NT + (k + 1))
                nc.vector.tensor_copy(attnT[:, k, :], e_bank[k % 2][:]).then_inc(attnT_odd, 1)

            def energy_max(b, n):
                dve.wait_ge(energy_filled, b * NT + (n + 1))
                nc.vector.reduce_max(col(neg_max, b * NT + n), e_bank[n % 2][:], axis=AX_X, negate=True
                                     ).then_inc(max_done, 1)

            def invert_sum(b, n):
                dve.wait_ge(exp_done, b * NT + (n + 1))
                nc.vector.reciprocal(col(inv_sum, b * NT + n), col(exp_sum, b * NT + n)).then_inc(inv_done, 1)

            def x1_rows(b, l):
                dve.wait_ge(mixed, b * LT + (l + 1))
                xr = row(x_all, b * LT + l)
                nc.vector.scalar_tensor_tensor(xr, m_bank[l % 2][:], 1.0 / H_SCALE, xr, ALU.mult, ALU.add
                                               ).then_inc(x1_done, 1)
            dve.wait_ge(x_here, 1)
            x_parts(0)
            dve.wait_ge(x_part, LT)
            statistics(0, 0)
            magic_numbers(0)
            for n in range(NT):
                energy_max(0, n)
                invert_sum(0, n)
            for m in range(3):
                round_weights(0, m)
            with dve.Fori(0, NB - 1) as b:
                dve.wait_ge(x_here, b + 2)
                copy_xT(b, 1)
                copy_xT(b, 3)
                copy_attnT(b, 1)
                copy_attnT(b, 3)
                x_parts(b + 1)
                dve.wait_ge(x_part, b * LT + 2 * LT)
                magic_numbers(b + 1)
                statistics(b + 1, 0)
                x1_rows(b, 0)
                dve.wait_ge(x1_done, b * LT + 1)
                round_weights(b + 1, 0)
                h_parts(b, 0)
                energy_max(b + 1, 0)
                energy_max(b + 1, 1)
                invert_sum(b + 1, 0)
                invert_sum(b + 1, 1)
                x1_rows(b, 1)
                dve.wait_ge(x1_done, b * LT + 2)
                energy_max(b + 1, 2)
                h_parts(b, 1)
                energy_max(b + 1, 3)
                invert_sum(b + 1, 2)
                invert_sum(b + 1, 3)
                x1_rows(b, 2)
                dve.wait_ge(x1_done, b * LT + 3)
                round_weights(b + 1, 1)
                h_parts(b, 2)
                x1_rows(b, 3)
                dve.wait_ge(x1_done, b * LT + 4)
                round_sum(b + 1, 2)
                h_parts(b, 3)
                dve.wait_ge(h_part, b * LT + LT)
                round_rest(b + 1, 2)
                statistics(b, 1)

            def copy_hT_lo(b, k, src):
                dve.wait_ge(hT_hi_done, b * KT + (k + 1))
                nc.vector.tensor_tensor(hT_lo[:, k, :], src[:], hT_hi[:, k, :], ALU.subtract
                                        ).then_inc(hT_lo_done, 1)

            last = NB - 1
            for k in range(1, KT, 2):
                copy_xT(last, k)
            for k in range(1, NT, 2):
                copy_attnT(last, k)
            for k in range(KT):
                copy_hT_lo(0, k, t_bank[k % 2])
            dve.wait_ge(down_s_landed, 16)
            nc.vector.tensor_scalar_mul(down_s[:], down_s[:], -1.0 / W_SHIFT).then_inc(down_s_done, 1)
            for l in range(LT):
                if l == 0:
                    magic_numbers(NB)
                x1_rows(last, l)
                dve.wait_ge(x1_done, last * LT + (l + 1))
                h_parts(last, l)
                if l < 3:
                    round_weights(NB, l)
            dve.wait_ge(h_part, NB * LT)
            statistics(last, 1)

            def fuse(b, j, q):
                n = b * IT + j * 2 + q
                dve.wait_ge(silu_done, n + 1)
                dve.wait_ge(up_filled, n + 1)
                nc.vector.scalar_tensor_tensor(fused[:, q, :], gu_bank[q][1][:], col(scales, j * 2 + (IT + q)),
                                               silu[:, q, :], ALU.mult, ALU.mult).then_inc(fused_done, 1)
                dve.wait_ge(f_hi_done, n + 1)
                nc.vector.tensor_tensor(f_lo[:, q, :], fused[:, q, :], f_hi[:, q, :].bitcast(F32), ALU.subtract
                                        ).then_inc(f_lo_done, 1)

            def scale_output(b, first):
                dve.wait_ge(down_done, b * IT + IT)
                if first:
                    dve.wait_ge(down_s_done, 1)
                if not first:
                    dve.wait_ge(out_landed, b * (16 * LT))
                for l in range(LT):
                    nc.vector.tensor_tensor(y[:, l, :], acc_bank[l][:], down_s[:], ALU.mult).then_inc(y_done, 1)

            for b in range(1):
                for j in range(NJ):
                    for q in range(2):
                        fuse(b, j, q)
                    if j < NJ - NB - 1:
                        magic_numbers(NB + 1 + j)
                        for m in range(3):
                            round_weights(NB + 1 + j, m)
                for k in range(KT):
                    copy_hT_lo(1, k, gu_bank[k // 2][k % 2])
                scale_output(0, True)
            with dve.Fori(1, NB - 1) as b:
                with dve.Fori(0, NJ) as j:
                    for q in range(2):
                        fuse(b, j, q)
                for k in range(KT):
                    copy_hT_lo(b + 1, k, gu_bank[k // 2][k % 2])
                scale_output(b, False)
            with dve.Fori(0, NJ) as j:
                for q in range(2):
                    fuse(last, j, q)
            scale_output(last, False)

        @block.scalar
        def _(act):
            def shift_weights(j, m):
                act.wait_ge(magic_done, j * 3 + (m + 1))
                nc.scalar.activation(raw[:, m, :], raw[:, m, :], ACT.Copy, scale=W_SHIFT).then_inc(shifted, 1)

            def copy_xT(b, k):
                act.wait_ge(normT_filled, b * KT + (k + 1))
                nc.scalar.activation(xT[:, k, :], t_bank[k % 2][:], ACT.Copy).then_inc(xT_even, 1)

            def copy_attnT(b, k):
                act.wait_ge(attnT_filled, b * NT + (k + 1))
                nc.scalar.activation(attnT[:, k, :], e_bank[k % 2][:], ACT.Copy).then_inc(attnT_even, 1)

            def copy_ctxT(b):
                for k in range(CT):
                    act.wait_ge(ctxT_filled, b * CT + (k + 1))
                    nc.scalar.activation(ctxT[:, k, :], c_bank[k][:], ACT.Copy).then_inc(ctxT_done, 1)

            def copy_qk(b):
                for i, dst in enumerate((qT, kT)):
                    act.wait_ge(qk_filled, b * 2 + (i + 1))
                    nc.scalar.activation(dst[:], c_bank[i][:], ACT.Identity, bias=bias[:, i:i + 1]
                                         ).then_inc(qk_done, 1)

            def exponentials(b, n):
                act.wait_ge(max_done, b * NT + (n + 1))
                nc.scalar.activation(attn[:, n, :], e_bank[n % 2][:], ACT.Exp,
                                     bias=col(neg_max, b * NT + n), accum_out=col(exp_sum, b * NT + n)
                                     ).then_inc(exp_done, 1)

            def normalise(b, n):
                act.wait_ge(inv_done, b * NT + (n + 1))
                nc.scalar.activation(attn[:, n, :], attn[:, n, :], ACT.Copy, scale=col(inv_sum, b * NT + n)).then_inc(attn_done, 1)

            def softmax(b, n0):
                exponentials(b, n0)
                exponentials(b, n0 + 1)
                normalise(b, n0)
                normalise(b, n0 + 1)

            def layernorm(b, kind, first=False):
                s = b + kind * NB
                act.wait_ge(ln_done[kind], b + (1 + kind))
                if not first:
                    act.wait_ge(normT_filled, s * KT)
                for l in range(LT):
                    nc.scalar.activation(norm[:, l, :], row(x_all, b * LT + l), ACT.Identity,
                                         bias=ln_shift[:, bass.ds(s, 1), l:l + 1].rearrange("p a n -> p (a n)"),
                                         scale=ln_scale[:, bass.ds(s, 1), l:l + 1].rearrange("p a n -> p (a n)")
                                         ).then_inc(norm_done, 1)

            act.wait_ge(wT_filled, 1)
            nc.scalar.activation(wT[:, :, :].rearrange("p t d -> p (t d)"), t_bank[0][:], ACT.Copy
                                 ).then_inc(wT_done, 1)
            act.wait_ge(scalesT_filled, 1)
            nc.scalar.activation(scales[:], t_bank[1][:, 0:2 * IT], ACT.Copy, scale=-1.0 / (W_SHIFT * H_SCALE)
                                 ).then_inc(wT_done, 1)
            copy_ctxT(0)
            act.wait_ge(small_landed, 96)
            copy_qk(0)
            softmax(0, 0)
            softmax(0, 2)
            layernorm(0, 0, True)
            for m in range(3):
                shift_weights(0, m)
            with act.Fori(0, NB - 1) as b:
                copy_ctxT(b + 1)
                for k in range(0, KT, 2):
                    copy_xT(b, k)
                for k in range(0, NT, 2):
                    copy_attnT(b, k)
                copy_qk(b + 1)
                layernorm(b + 1, 0)
                for m in range(3):
                    shift_weights(b + 1, m)
                act.wait_ge(attnT_filled, b * NT + NT)
                softmax(b + 1, 0)
                softmax(b + 1, 2)

            def copy_hT_hi(b, k, src):
                act.wait_ge(normT_filled, b * KT + (NB * KT + k + 1))
                nc.scalar.activation(hT_hi[:, k, :], src[:], ACT.Copy).then_inc(hT_hi_done, 1)

            for k in range(0, KT, 2):
                copy_xT(NB - 1, k)
            for k in range(0, NT, 2):
                copy_attnT(NB - 1, k)
            layernorm(0, 1)
            for k in range(KT):
                copy_hT_hi(0, k, t_bank[k % 2])
            for m in range(3):
                shift_weights(NB, m)

            def gate_silu(b, j, q):
                n = b * IT + j * 2 + q
                act.wait_ge(gate_filled, n + 1)
                nc.scalar.activation(silu[:, q, :], gu_bank[q][0][:], ACT.Silu, scale=col(scales, j * 2 + q)
                                     ).then_inc(silu_done, 1)
                act.wait_ge(fused_done, n + 1)
                nc.scalar.activation(f_hi[:, q, :], fused[:, q, :], ACT.Copy).then_inc(f_hi_done, 1)

            for j in range(NJ):
                for q in range(2):
                    gate_silu(0, j, q)
                if j == 0:
                    layernorm(1, 1)
                if j < NJ - NB - 1:
                    for m in range(3):
                        shift_weights(NB + 1 + j, m)
            for k in range(KT):
                copy_hT_hi(1, k, gu_bank[k // 2][k % 2])
            with act.Fori(1, NB - 1) as b:
                for q in range(2):
                    gate_silu(b, 0, q)
                layernorm(b + 1, 1)
                with act.Fori(1, NJ) as j:
                    for q in range(2):
                        gate_silu(b, j, q)
                for k in range(KT):
                    copy_hT_hi(b + 1, k, gu_bank[k // 2][k % 2])
            with act.Fori(0, NJ) as j:
                for q in range(2):
                    gate_silu(NB - 1, j, q)

        @block.tensor
        def _(pe):
            mm = nc.tensor.matmul

            def transpose_ctx(b):
                pe.wait_ge(ctx_here, b + 1)
                for k in range(CT):
                    for n in range(NT):
                        t = nc.tensor.transpose(c_bank[k][:, n * P:(n + 1) * P],
                                                ctx_in[:, n, k * P:(k + 1) * P], ident[:])
                    t.then_inc(ctxT_filled, 1)

            def project(b):
                pe.wait_ge(ctxT_done, b * CT + CT)
                for i in range(2):
                    for k in range(CT):
                        t = mm(c_bank[i][:], wT[:, i * CT + k, :], ctxT[:, k, :],
                               start=(k == 0), stop=(k == CT - 1))
                    t.then_inc(qk_filled, 1)

            def energies(b, n, first):
                if n == 0:
                    pe.wait_ge(qk_done, b * 2 + 2)
                if n >= 2:
                    pe.wait_ge(exp_done, b * NT + (n - 1))
                elif not first:
                    pe.wait_ge([attnT_even, attnT_odd][n], b * 2)
                mm(e_bank[n % 2][:], qT[:, n * P:(n + 1) * P], kT[:], start=True, stop=True
                   ).then_inc(energy_filled, 1)

            def transpose_rows(s, k, dst):
                for l in range(LT):
                    t = nc.tensor.transpose(dst[:, l * P:(l + 1) * P], norm[:, l, k * P:(k + 1) * P], ident[:])
                t.then_inc(normT_filled, 1)

            def transpose_x(b, first):
                pe.wait_ge(norm_done, b * LT + LT)
                for k in range(KT):
                    if k >= 2 or not first:
                        done = xT_even if k % 2 == 0 else xT_odd
                        pe.wait_ge(done, b * 2 + k // 2)
                    transpose_rows(b, k, t_bank[k % 2])

            def transpose_attn(b):
                pe.wait_ge(attn_done, b * NT + NT)
                for k in range(NT):
                    if k >= 2:
                        pe.wait_ge([attnT_even, attnT_odd][k % 2], b * 2 + 1)
                    for n in range(NT):
                        t = nc.tensor.transpose(e_bank[k % 2][:, n * P:(n + 1) * P],
                                                attn[:, n, k * P:(k + 1) * P], ident[:])
                    t.then_inc(attnT_filled, 1)

            def mix(b, l, first):
                if l == 0:
                    pe.wait_ge(xT_even, b * 2 + 2)
                    pe.wait_ge(xT_odd, b * 2 + 2)
                    pe.wait_ge(attnT_even, b * 2 + 2)
                    pe.wait_ge(attnT_odd, b * 2 + 2)
                if not (first and l < 2):
                    pe.wait_ge(x1_done, b * LT + (l - 1))
                for k in range(KT):
                    t = mm(m_bank[l % 2][:], xT[:, k, l * P:(l + 1) * P], attnT[:, k, :],
                           start=(k == 0), stop=(k == KT - 1))
                t.then_inc(mixed, 1)

            pe.wait_ge(consts_done, 2)
            pe.wait_ge(small_landed, 96)
            for i in range(2):
                for k in range(CT):
                    at = (i * CT + k) * P
                    t = nc.tensor.transpose(t_bank[0][:, at:at + P], w_in[:, i, k * P:(k + 1) * P], ident[:])
            t.then_inc(wT_filled, 1)
            nc.tensor.transpose(t_bank[1][:, 0:2 * IT], scales_in[:], ident[0:2 * IT, 0:2 * IT]
                                ).then_inc(scalesT_filled, 1)
            transpose_ctx(0)
            pe.wait_ge(wT_done, 2)
            project(0)
            for n in range(NT):
                energies(0, n, True)

            def attention(b, first):
                transpose_ctx(b + 1)
                transpose_x(b, first)
                transpose_attn(b)
                project(b + 1)
                mix(b, 0, first)
                energies(b + 1, 0, False)
                energies(b + 1, 1, False)
                mix(b, 1, first)
                energies(b + 1, 2, False)
                energies(b + 1, 3, False)
                mix(b, 2, first)
                mix(b, 3, first)

            attention(0, True)
            with pe.Fori(1, NB - 1) as b:
                attention(b, False)
            transpose_x(NB - 1, False)
            transpose_attn(NB - 1)
            pe.wait_ge(norm_done, NB * LT + LT)
            for k in range(KT):
                if k < 2:
                    pe.wait_ge(xT_even if k % 2 == 0 else xT_odd, NB * 2)
                else:
                    pe.wait_ge(hT_lo_done, k - 1)
                transpose_rows(NB, k, t_bank[k % 2])
            for l in range(LT):
                mix(NB - 1, l, False)

            def gate_up(b, j, q, free):
                if free is not None:
                    pe.wait_ge(fused_done, free)
                for w, dst, filled in ((gate_q, gu_bank[q][0], gate_filled), (up_q, gu_bank[q][1], up_filled)):
                    for k in range(KT):
                        lhsT = w[:, bass.ds(j, 1), k, q * P:(q + 1) * P].rearrange("p a c -> p (a c)")
                        mm(dst[:], lhsT, hT_hi[:, k, :], start=(k == 0), stop=False)
                        t = mm(dst[:], lhsT, hT_lo[:, k, :], start=False, stop=(k == KT - 1))
                    t.then_inc(filled, 1)

            def down(b, j, q):
                n = b * IT + j * 2 + q
                pe.wait_ge(f_lo_done, n + 1)
                start = isinstance(j, int) and j == 0 and q == 0
                stop = isinstance(j, int) and j == NJ - 1 and q == 1
                rhs = down_q[:, bass.ds(j, 1), q, :].rearrange("p a c -> p (a c)")
                for l in range(LT):
                    mm(acc_bank[l][:], f_hi[:, q, l * P:(l + 1) * P], rhs, start=start, stop=False)
                    t = mm(acc_bank[l][:], f_lo[:, q, l * P:(l + 1) * P], rhs, start=False, stop=stop)
                t.then_inc(down_done, 1)

            def ffn(b, nexth):
                pe.wait_ge(hT_lo_done, b * KT + KT)
                pe.wait_ge(weights_done, 3)
                gate_up(b, 0, 0, None)
                gate_up(b, 0, 1, None)
                if isinstance(b, int) and b == 0:
                    pe.wait_ge(x1_done, NB * LT)
                else:
                    pe.wait_ge(y_done, b * LT)
                down(b, 0, 0)
                with pe.Fori(1, NJ) as j:
                    pe.wait_ge(weights_done, j * 3 + 3)
                    n = b * IT + j * 2
                    gate_up(b, j, 0, n - 1)
                    down(b, j - 1, 1)
                    gate_up(b, j, 1, n)
                    down(b, j, 0)
                if nexth:
                    pe.wait_ge(norm_done, b * LT + (NB * LT + 2 * LT))
                    for k in range(KT):
                        if k % 2 == 0:
                            pe.wait_ge(fused_done, b * IT + (IT - 1 + k // 2))
                        transpose_rows(0, k, gu_bank[k // 2][k % 2])
                down(b, NJ - 1, 1)

            ffn(0, True)
            with pe.Fori(1, NB - 1) as b:
                ffn(b, True)
            ffn(NB - 1, False)


_INPUTS = {
    "x": "x", "ctx_tokens": "ctx_1024", "wq": "L0_xattn_Wq", "bq": "L0_xattn_bq", "wk": "L0_xattn_Wk",
    "bk": "L0_xattn_bk", "gate_w": "L0_ffn_gate_w", "up_w": "L0_ffn_up_w", "down_w": "L0_ffn_down_w",
    "gate_scale": "L0_ffn_gate_scale", "up_scale": "L0_ffn_up_scale", "down_scale": "L0_ffn_down_scale",
}


def kernel(**inputs):
    import numpy as np
    import concourse.bacc as bacc
    from concourse.bass_utils import run_bass_kernel_spmd

    nc = bacc.Bacc("TRN2", target_bir_lowering=False, num_devices=1)
    arrays, aps = {}, {}
    for name, key in _INPUTS.items():
        a = np.ascontiguousarray(inputs[key])
        arrays[f"in_{name}"] = a
        aps[name] = nc.dram_tensor(f"in_{name}", a.shape, mybir.dt.from_np(a.dtype), kind="ExternalInput").ap()
    out = nc.dram_tensor("out_x", arrays["in_x"].shape, F32, kind="ExternalOutput").ap()
    build_xattn_ffn(nc, out=out, **aps)
    result = run_bass_kernel_spmd(nc, [arrays], core_ids=[0])
    return result.results[0]["out_x"]
```

```python
from contextlib import ExitStack

import concourse.bass as bass
from concourse import mybir

F32 = mybir.dt.float32
F32R = mybir.dt.float32r
F16 = mybir.dt.float16
BF16 = mybir.dt.bfloat16
I32 = mybir.dt.int32
ALU = mybir.AluOpType
ACT = mybir.ActivationFunctionType
AX_X = mybir.AxisListType.X

P = 128
WARM_UP = 16
LN_EPS = 1e-5
H_SCALE = 2.0 ** 11
W_SHIFT = 2.0 ** -20
EXPONENT_BITS = 0x7F800000
HALF_BIT = 0x00400000
FLOOR = 1.5 * 2.0 ** -6


def build_xattn_ffn(nc, x, ctx_tokens, wq, bq, wk, bk, gate_w, up_w, down_w,
                    gate_scale, up_scale, down_scale, out):
    NB, L, H = x.shape
    N, C = ctx_tokens.shape[1:]
    D = wq.shape[0]
    I = gate_w.shape[1]
    LT, KT, NT, CT, IT = L // P, H // P, N // P, C // P, I // P
    NJ = IT // 2
    assert D == P and N == H and L == 512 and H == 512 and LT == KT == NT == 4 and CT == 2
    assert IT % 2 == 0 and NB + 2 == NJ

    x_rows = x.rearrange("b (l p) h -> b p l h", p=P)
    out_rows = out.rearrange("b (l p) h -> b p l h", p=P)
    ctx_rows = ctx_tokens.rearrange("b (n p) c -> b p n c", p=P)
    gate_cols = gate_w.rearrange("(k p) (j c) -> j p k c", p=P, c=2 * P)
    up_cols = up_w.rearrange("(k p) (j c) -> j p k c", p=P, c=2 * P)
    down_rows = down_w.rearrange("(j t p) h -> j p t h", p=P, t=2)

    with ExitStack() as stack:
        def sb(name, shape, dt):
            return stack.enter_context(nc.sbuf_tensor(name, shape, dt))

        def sem(name):
            return stack.enter_context(nc.semaphore(name))

        x_all = sb("x_all", [P, NB * LT, H], F32)
        ctx_in = sb("ctx_in", [P, NT, C], F32)
        w_in = sb("w_in", [P, 2, C], F32)
        wT = sb("wT", [P, 2 * CT, D], F32)
        bias = sb("bias", [P, 2], F32)
        ident = sb("ident", [P, P], F32)
        norm = sb("norm", [P, LT, H], F32)
        xT = sb("xT", [P, KT, L], F32)
        ctxT = sb("ctxT", [P, CT, N], F32)
        qT = sb("qT", [P, N], F32)
        kT = sb("kT", [P, N], F32)
        attn = sb("attn", [P, NT, H], F32)
        attnT = sb("attnT", [P, NT, H], F32)
        part = sb("part", [P, 2 * LT, 6], F32)
        meanvar = sb("meanvar", [P, 2 * LT, 2], F32)
        ln_var = sb("ln_var", [P, 2, LT], F32)
        ln_mean = sb("ln_mean", [P, 2, LT], F32)
        ln_scale = sb("ln_scale", [P, 2 * NB, LT], F32)
        ln_shift = sb("ln_shift", [P, 2 * NB, LT], F32)
        minus_half = sb("minus_half", [P, LT], F32)
        neg_max = sb("neg_max", [P, NB * NT], F32)
        exp_sum = sb("exp_sum", [P, NB * NT], F32)
        inv_sum = sb("inv_sum", [P, NB * NT], F32)
        raw = sb("raw", [P, 2 * 3, 1024], F32)
        magic = sb("magic", [P, 3, 1024], F32)
        gate_q = sb("gate_q", [P, NJ, KT, 2 * P], BF16)
        up_q = sb("up_q", [P, NJ, KT, 2 * P], BF16)
        down_q = sb("down_q", [P, NJ, 2, H], F32R)
        scales_in = sb("scales_in", [2 * IT, P], F32)
        scales = sb("scales", [P, 2 * IT], F32)
        down_s = sb("down_s", [P, H], F32)
        hT_hi = sb("hT_hi", [P, KT, L], F16)
        hT_lo = sb("hT_lo", [P, KT, L], F16)
        silu = sb("silu", [P, 2, L], F32)
        fused = sb("fused", [P, 2, L], F32)
        f_hi = sb("f_hi", [P, 2, L], F32R)
        f_lo = sb("f_lo", [P, 2, L], F32R)
        y = sb("y", [P, LT, H], F32)

        bank = [stack.enter_context(nc.psum_tensor(f"bank{i}", [P, 512], F32)) for i in range(8)]
        t_bank, m_bank, e_bank, c_bank = bank[0:2], bank[2:4], bank[4:6], bank[6:8]
        xT_bank = bank[0:4]
        attnT_bank = bank[4:6] + bank[0:2]
        acc_bank = bank[0:4]
        gu_bank = [bank[4:6], bank[6:8]]

        w_landed = sem("w_landed")
        small_landed = sem("small_landed")
        down_s_landed = sem("down_s_landed")
        x_landed = [sem(f"x_landed{b}") for b in range(NB)]
        ctx_landed = [sem(f"ctx_landed{b}") for b in range(NB)]
        raw_landed = [sem(f"raw_landed{j}") for j in range(NJ)]
        x_here = sem("x_here")
        ctx_here = sem("ctx_here")
        raw_here = sem("raw_here")
        consts_step = sem("consts_step")
        consts_done = sem("consts_done")
        down_s_done = sem("down_s_done")
        wT_filled, wT_done = sem("wT_filled"), sem("wT_done")
        scalesT_filled, scales_done = sem("scalesT_filled"), sem("scales_done")
        x_part, x_stats = sem("x_part"), sem("x_stats")
        h_part, h_stats = sem("h_part"), sem("h_stats")
        moments = [sem("x_moments"), sem("h_moments")]
        ln_step = [sem("x_ln_step"), sem("h_ln_step")]
        ln_done = [sem("x_ln_done"), sem("h_ln_done")]
        norm_done = sem("norm_done")
        normT_filled = sem("normT_filled")
        xT_done = sem("xT_done")
        ctxT_filled, ctxT_done = sem("ctxT_filled"), sem("ctxT_done")
        qk_filled, qk_done = sem("qk_filled"), sem("qk_done")
        energy_filled = sem("energy_filled")
        max_done, exp_done = sem("max_done"), sem("exp_done")
        inv_done, attn_done = sem("inv_done"), sem("attn_done")
        attnT_filled = sem("attnT_filled")
        attnT_done = sem("attnT_done")
        mixed = sem("mixed")
        x1_done = sem("x1_done")
        magic_done, shifted, summed = sem("magic_done"), sem("shifted"), sem("summed")
        weights_done = sem("weights_done")
        hT_hi_done, hT_lo_done = sem("hT_hi_done"), sem("hT_lo_done")
        gate_filled, up_filled = sem("gate_filled"), sem("up_filled")
        silu_done, fused_done = sem("silu_done"), sem("fused_done")
        f_hi_done, f_lo_done = sem("f_hi_done"), sem("f_lo_done")
        f_free = sem("f_free")
        acc_done = sem("acc_done")
        y_done, out_done = sem("y_done"), sem("out_done")
        odd_y_done = sem("odd_y_done")
        odd_out_done = sem("odd_out_done")
        out_landed = sem("out_landed")

        def row(buf, i):
            return buf[:, bass.ds(i, 1), :].rearrange("p a n -> p (a n)")

        def col(buf, i):
            return buf[:, bass.ds(i, 1)]

        block = stack.enter_context(nc.Block())

        @block.sync
        def _(sp):
            raw_src = [gate_cols, up_cols, down_rows]

            def load_weights(j):
                for m in range(3):
                    dst = raw[:, (j % 2) * 3 + m, :].rearrange("p (k c) -> p k c", k=raw_src[m].shape[2])
                    sp.dma_start(dst, raw_src[m][j]).then_inc(raw_landed[j], 16)

            def load_x(b):
                sp.dma_start(x_all[:, b * LT:(b + 1) * LT, :], x_rows[b]).then_inc(x_landed[b], 16)

            def load_ctx(b):
                sp.dma_start(ctx_in[:], ctx_rows[b]).then_inc(ctx_landed[b], 16)

            def pass_on(landed, value, here):
                sp.wait_ge(landed, value)
                sp.sem_inc(here, 1)

            sp.dma_start(w_in[:, 0, :], wq).then_inc(w_landed, 16)
            sp.dma_start(w_in[:, 1, :], wk).then_inc(w_landed, 16)
            load_ctx(0)
            load_x(0)
            sp.dma_start(bias[:, 0:1], bq.rearrange("(p a) -> p a", a=1)).then_inc(small_landed, 16)
            sp.dma_start(bias[:, 1:2], bk.rearrange("(p a) -> p a", a=1)).then_inc(small_landed, 16)
            sp.dma_start(scales_in[0:IT, :], gate_scale.rearrange("(i p) -> i p", p=P)).then_inc(small_landed, 16)
            sp.dma_start(scales_in[IT:2 * IT, :], up_scale.rearrange("(i p) -> i p", p=P)
                         ).then_inc(small_landed, 16)
            pass_on(ctx_landed[0], 16, ctx_here)
            sp.wait_ge(ctxT_filled, CT)
            load_ctx(1)
            load_weights(0)
            load_x(1)
            load_weights(1)
            sp.dma_start(down_s[:], down_scale.rearrange("(a h) -> a h", a=1).broadcast_to([P, H])
                         ).then_inc(down_s_landed, 16)
            pass_on(x_landed[0], 16, x_here)
            pass_on(ctx_landed[1], 16, ctx_here)
            pass_on(raw_landed[0], 48, raw_here)
            pass_on(x_landed[1], 16, x_here)
            for b in range(2, NB):
                sp.wait_ge(ctxT_filled, CT * b)
                load_ctx(b)
                load_x(b)
                if b == 2:
                    pass_on(raw_landed[1], 48, raw_here)
                pass_on(ctx_landed[b], 16, ctx_here)
                pass_on(x_landed[b], 16, x_here)
                sp.wait_ge(weights_done, 3 * (b - 1))
                load_weights(b)
                pass_on(raw_landed[b], 48, raw_here)
            for j in range(NB, NJ):
                sp.wait_ge(weights_done, 3 * (j - 1))
                load_weights(j)
                pass_on(raw_landed[j], 48, raw_here)
            with sp.Fori(0, NB - 1) as b:
                for l in range(LT):
                    sp.wait_ge(out_done, b * LT + (l + 1))
                    sp.dma_start(out_rows[bass.ds(b, 1), :, l, :].rearrange("a p h -> (a p) h"), y[:, l, :]
                                 ).then_inc(out_landed, 16)
            for l in range(LT):
                if l % 2 == 0:
                    sp.wait_ge(out_done, (NB - 1) * LT + (l // 2 + 1))
                else:
                    sp.wait_ge(odd_out_done, l // 2 + 1)
                sp.dma_start(out_rows[NB - 1, :, l, :], y[:, l, :]).then_inc(out_landed, 16)
            sp.wait_ge(out_landed, 16 * NB * LT)

        @block.gpsimd
        def _(pool):
            nc.gpsimd.memset(ident[:], 0.0).then_inc(consts_step, 1)
            pool.wait_ge(consts_step, 1)
            nc.gpsimd.affine_select(out=ident[:], in_=ident[:], compare_op=ALU.not_equal, fill=1.0, base=0,
                                    pattern=[[-1, P]], channel_multiplier=1).then_inc(consts_done, 1)
            nc.gpsimd.memset(minus_half[:], -0.5).then_inc(consts_done, 1)
            pool.wait_ge(consts_done, 2)
            pool.sem_inc(ln_done[1], 1)

            def ln_factors(b, kind):
                s = b + kind * NB
                pool.wait_ge(moments[kind], b * 2 + 2)
                nc.gpsimd.tensor_tensor(row(ln_scale, s), ln_var[:, kind, :], minus_half[:], ALU.pow
                                        ).then_inc(ln_step[kind], 1)
                pool.wait_ge(ln_step[kind], b + 1)
                nc.gpsimd.tensor_tensor(row(ln_shift, s), ln_mean[:, kind, :], row(ln_scale, s), ALU.mult
                                        ).then_inc(ln_done[kind], 1)

            ln_factors(0, 0)
            with pool.Fori(0, NB - 1) as b:
                ln_factors(b + 1, 0)
                ln_factors(b, 1)
            ln_factors(NB - 1, 1)

            def add_residual(b):
                for l in range(LT):
                    pool.wait_ge(y_done, b * LT + (l + 1))
                    nc.gpsimd.tensor_tensor(y[:, l, :], y[:, l, :], row(x_all, b * LT + l), ALU.add
                                            ).then_inc(out_done, 1)

            with pool.Fori(0, NB - 1) as b:
                add_residual(b)
            for i in range(LT // 2):
                pool.wait_ge(y_done, (NB - 1) * LT + (i + 1))
                nc.gpsimd.tensor_tensor(y[:, 2 * i, :], y[:, 2 * i, :], x_all[:, (NB - 1) * LT + 2 * i, :], ALU.add
                                        ).then_inc(out_done, 1)

        @block.vector
        def _(dve):
            def x_parts(b):
                for l in range(LT):
                    nc.vector.bn_stats(part[:, l, :], row(x_all, b * LT + l)).then_inc(x_part, 1)

            def h_parts(b, l):
                nc.vector.bn_stats(part[:, LT + l, :], row(x_all, b * LT + l)).then_inc(h_part, 1)

            def statistics(b, kind):
                stats = [x_stats, h_stats][kind]
                for l in range(LT):
                    nc.vector.bn_aggr(meanvar[:, kind * LT + l, :], part[:, kind * LT + l, :]).then_inc(stats, 1)
                if kind or not isinstance(b, int) or b:
                    dve.wait_ge(ln_done[kind], b + kind)
                dve.wait_ge(stats, b * LT + LT)
                mv = meanvar[:, kind * LT:(kind + 1) * LT, :]
                nc.vector.tensor_scalar(ln_var[:, kind, :], mv[:, :, 1], LN_EPS, H_SCALE ** -2, ALU.add, ALU.mult
                                        ).then_inc(moments[kind], 1)
                nc.vector.tensor_scalar_mul(ln_mean[:, kind, :], mv[:, :, 0], -1.0).then_inc(moments[kind], 1)

            def magic_numbers(j, ms=range(3)):
                for m in ms:
                    if m == 0:
                        if not isinstance(j, int) or j:
                            dve.wait_ge(weights_done, j * 3)
                        dve.wait_ge(raw_here, j + 1)
                    nc.vector.tensor_scalar(magic[:, m, :].bitcast(I32), row(raw, (j % 2) * 3 + m).bitcast(I32),
                                            EXPONENT_BITS, HALF_BIT, ALU.bitwise_and, ALU.bitwise_or
                                            ).then_inc(magic_done, 1)

            def round_weights(j, m):
                w = row(raw, (j % 2) * 3 + m)
                dve.wait_ge(shifted, j * 3 + (m + 1))
                nc.vector.scalar_tensor_tensor(w, magic[:, m, :], FLOOR, w, ALU.max, ALU.add).then_inc(summed, 1)
                dst = [gate_q, up_q, down_q][m][:, bass.ds(j, 1), :, :].rearrange("p a k c -> p (a k c)")
                dve.wait_ge(summed, j * 3 + (m + 1))
                nc.vector.scalar_tensor_tensor(dst, magic[:, m, :], FLOOR, w, ALU.max, ALU.subtract
                                               ).then_inc(weights_done, 1)

            def energy_max(b, n):
                dve.wait_ge(energy_filled, b * NT + (n + 1))
                nc.vector.reduce_max(col(neg_max, b * NT + n), e_bank[n % 2][:], axis=AX_X, negate=True
                                     ).then_inc(max_done, 1)

            def invert_sum(b, n):
                dve.wait_ge(exp_done, b * NT + (n + 1))
                nc.vector.reciprocal(col(inv_sum, b * NT + n), col(exp_sum, b * NT + n)).then_inc(inv_done, 1)

            def x1_rows(b, l):
                dve.wait_ge(mixed, b * LT + (l + 1))
                xr = row(x_all, b * LT + l)
                nc.vector.scalar_tensor_tensor(xr, m_bank[l % 2][:], 1.0 / H_SCALE, xr, ALU.mult, ALU.add
                                               ).then_inc(x1_done, 1)

            dve.wait_ge(wT_filled, 1)
            nc.vector.tensor_copy(wT[:, :, :].rearrange("p t d -> p (t d)"), t_bank[0][:]).then_inc(wT_done, 1)
            dve.wait_ge(x_landed[0], 16)
            x_parts(0)
            dve.wait_ge(x_part, LT)
            statistics(0, 0)
            energy_max(0, 0)
            energy_max(0, 1)
            dve.wait_ge(scalesT_filled, 1)
            nc.vector.tensor_scalar_mul(scales[:], t_bank[1][:, 0:2 * IT], -1.0 / (W_SHIFT * H_SCALE)
                                        ).then_inc(scales_done, 1)
            invert_sum(0, 0)
            dve.wait_ge(ln_done[0], 1)
            for l in range(LT):
                nc.vector.tensor_scalar(norm[:, l, :], x_all[:, l, :], ln_scale[:, 0, l:l + 1],
                                        ln_shift[:, 0, l:l + 1], ALU.mult, ALU.add).then_inc(norm_done, 1)
            invert_sum(0, 1)
            energy_max(0, 2)
            energy_max(0, 3)
            invert_sum(0, 2)
            invert_sum(0, 3)

            def attention(b, first):
                if not first:
                    x1_rows(b - 1, 3)
                    dve.wait_ge(x1_done, b * LT)
                dve.wait_ge(x_here, b + 2)
                magic_numbers(b, (0,))
                if not first:
                    h_parts(b - 1, 3)
                    dve.wait_ge(h_part, b * LT)
                magic_numbers(b, (1,))
                if not first:
                    statistics(b - 1, 1)
                x_parts(b + 1)
                dve.wait_ge(x_part, b * LT + 2 * LT)
                magic_numbers(b, (2,))
                statistics(b + 1, 0)
                round_weights(b, 0)
                if not first:
                    round_weights(b, 1)
                x1_rows(b, 0)
                dve.wait_ge(x1_done, b * LT + 1)
                energy_max(b + 1, 0)
                energy_max(b + 1, 1)
                invert_sum(b + 1, 0)
                h_parts(b, 0)
                invert_sum(b + 1, 1)
                if first:
                    round_weights(b, 1)
                x1_rows(b, 1)
                dve.wait_ge(x1_done, b * LT + 2)
                energy_max(b + 1, 2)
                energy_max(b + 1, 3)
                invert_sum(b + 1, 2)
                h_parts(b, 1)
                invert_sum(b + 1, 3)
                x1_rows(b, 2)
                dve.wait_ge(x1_done, b * LT + 3)
                round_weights(b, 2)
                h_parts(b, 2)

            attention(0, True)
            with dve.Fori(1, NB - 1) as b:
                attention(b, False)

            def copy_hT_lo(b, k, src):
                dve.wait_ge(hT_hi_done, b * KT + (k + 1))
                nc.vector.tensor_tensor(hT_lo[:, k, :], src[:], hT_hi[:, k, :], ALU.subtract
                                        ).then_inc(hT_lo_done, 1)

            last = NB - 1
            x1_rows(last - 1, 3)
            magic_numbers(last)
            dve.wait_ge(x1_done, last * LT)
            h_parts(last - 1, 3)
            dve.wait_ge(h_part, last * LT)
            statistics(last - 1, 1)
            round_weights(last, 0)
            for l in range(LT):
                x1_rows(last, l)
                dve.wait_ge(x1_done, last * LT + (l + 1))
                h_parts(last, l)
                if l == 1:
                    for k in range(KT):
                        copy_hT_lo(0, k, attnT_bank[k])
                if l == 0:
                    round_weights(last, 1)
            dve.wait_ge(h_part, NB * LT)
            statistics(last, 1)
            dve.wait_ge(down_s_landed, 16)
            nc.vector.tensor_scalar_mul(down_s[:], down_s[:], -1.0 / W_SHIFT).then_inc(down_s_done, 1)

            def fuse(b, j, q):
                n = b * IT + j * 2 + q
                dve.wait_ge(silu_done, n + 1)
                dve.wait_ge(up_filled, n + 1)
                nc.vector.scalar_tensor_tensor(fused[:, q, :], gu_bank[q][1][:], col(scales, j * 2 + (IT + q)),
                                               silu[:, q, :], ALU.mult, ALU.mult).then_inc(fused_done, 1)
                dve.wait_ge(f_hi_done, n + 1)
                nc.vector.tensor_tensor(f_lo[:, q, :], fused[:, q, :], f_hi[:, q, :].bitcast(F32), ALU.subtract
                                        ).then_inc(f_lo_done, 1)

            def scale_output(b, first):
                if first:
                    dve.wait_ge(down_s_done, 1)
                if not first:
                    dve.wait_ge(out_landed, b * (16 * LT))
                for l in range(LT):
                    dve.wait_ge(acc_done, b * LT + (l + 1))
                    nc.vector.tensor_tensor(y[:, l, :], acc_bank[l][:], down_s[:], ALU.mult).then_inc(y_done, 1)

            for n in range(8):
                fuse(0, n // 2, n % 2)
                if n == 0:
                    round_weights(last, 2)
                elif n == 1:
                    magic_numbers(NB)
                elif n < 5:
                    round_weights(NB, n - 2)
                else:
                    round_weights(NB + 1, n - 5)
                if n == 4:
                    magic_numbers(NB + 1)
            with dve.Fori(4, NJ) as j:
                for q in range(2):
                    fuse(0, j, q)
            for k in range(KT):
                copy_hT_lo(1, k, gu_bank[k // 2][k % 2])
            scale_output(0, True)
            with dve.Fori(1, NB - 1) as b:
                with dve.Fori(0, NJ) as j:
                    for q in range(2):
                        fuse(b, j, q)
                for k in range(KT):
                    copy_hT_lo(b + 1, k, gu_bank[k // 2][k % 2])
                scale_output(b, False)
            with dve.Fori(0, NJ) as j:
                for q in range(2):
                    fuse(last, j, q)
            dve.wait_ge(out_landed, last * (16 * LT))

            def scale_last(l):
                dve.wait_ge(acc_done, last * LT + (l + 1))
                nc.vector.tensor_tensor(y[:, l, :], acc_bank[l][:], down_s[:], ALU.mult
                                        ).then_inc([y_done, odd_y_done][l % 2], 1)

            def add_residual(l):
                dve.wait_ge(odd_y_done, l // 2 + 1)
                nc.vector.tensor_tensor(y[:, l, :], y[:, l, :], x_all[:, last * LT + l, :], ALU.add
                                        ).then_inc(odd_out_done, 1)

            scale_last(0)
            scale_last(1)
            scale_last(2)
            add_residual(1)
            scale_last(3)
            add_residual(3)

        @block.scalar
        def _(act):
            def shift_weights(j, m):
                act.wait_ge(magic_done, j * 3 + (m + 1))
                w = row(raw, (j % 2) * 3 + m)
                nc.scalar.activation(w, w, ACT.Copy, scale=W_SHIFT).then_inc(shifted, 1)

            def copy_xT(b, k):
                act.wait_ge(normT_filled, b * KT + (k + 1))
                nc.scalar.activation(xT[:, k, :], xT_bank[k][:], ACT.Copy).then_inc(xT_done, 1)

            def copy_attnT(b, k):
                act.wait_ge(attnT_filled, b * NT + (k + 1))
                nc.scalar.activation(attnT[:, k, :], attnT_bank[k][:], ACT.Copy).then_inc(attnT_done, 1)

            def copy_ctxT(b):
                for k in range(CT):
                    act.wait_ge(ctxT_filled, b * CT + (k + 1))
                    nc.scalar.activation(ctxT[:, k, :], c_bank[k][:], ACT.Copy).then_inc(ctxT_done, 1)

            def copy_qk(b, i):
                act.wait_ge(qk_filled, b * 2 + (i + 1))
                nc.scalar.activation([qT, kT][i][:], c_bank[i][:], ACT.Identity, bias=bias[:, i:i + 1]
                                     ).then_inc(qk_done, 1)

            def exponentials(b, n):
                act.wait_ge(max_done, b * NT + (n + 1))
                nc.scalar.activation(attn[:, n, :], e_bank[n % 2][:], ACT.Exp,
                                     bias=col(neg_max, b * NT + n), accum_out=col(exp_sum, b * NT + n)
                                     ).then_inc(exp_done, 1)

            def normalise(b, n):
                act.wait_ge(inv_done, b * NT + (n + 1))
                nc.scalar.activation(attn[:, n, :], attn[:, n, :], ACT.Copy, scale=col(inv_sum, b * NT + n)).then_inc(attn_done, 1)

            def softmax(b, n0):
                exponentials(b, n0)
                exponentials(b, n0 + 1)
                normalise(b, n0)
                normalise(b, n0 + 1)

            def layernorm(b, kind):
                s = b + kind * NB
                act.wait_ge(ln_done[kind], b + (1 + kind))
                act.wait_ge(normT_filled, s * KT)
                for l in range(LT):
                    nc.scalar.activation(norm[:, l, :], row(x_all, b * LT + l), ACT.Identity,
                                         bias=ln_shift[:, bass.ds(s, 1), l:l + 1].rearrange("p a n -> p (a n)"),
                                         scale=ln_scale[:, bass.ds(s, 1), l:l + 1].rearrange("p a n -> p (a n)")
                                         ).then_inc(norm_done, 1)

            copy_ctxT(0)
            act.wait_ge(small_landed, 64)
            copy_qk(0, 0)
            copy_qk(0, 1)
            softmax(0, 0)
            copy_ctxT(1)
            softmax(0, 2)

            def attention(b, first):
                if not first:
                    copy_ctxT(b + 1)
                for k in range(KT):
                    copy_xT(b, k)
                if not first:
                    shift_weights(b, 0)
                copy_qk(b + 1, 0)
                if not first:
                    shift_weights(b, 1)
                    copy_qk(b + 1, 1)
                for k in range(NT):
                    copy_attnT(b, k)
                if first:
                    copy_qk(b + 1, 1)
                    shift_weights(b, 0)
                    shift_weights(b, 1)
                layernorm(b + 1, 0)
                shift_weights(b, 2)
                softmax(b + 1, 0)
                softmax(b + 1, 2)

            attention(0, True)
            with act.Fori(1, NB - 1) as b:
                attention(b, False)

            def copy_hT_hi(b, k, src):
                act.wait_ge(normT_filled, b * KT + (NB * KT + k + 1))
                nc.scalar.activation(hT_hi[:, k, :], src[:], ACT.Copy).then_inc(hT_hi_done, 1)

            for k in range(KT):
                copy_xT(NB - 1, k)
            for k in range(NT):
                copy_attnT(NB - 1, k)
            layernorm(0, 1)
            for m in range(3):
                shift_weights(NB - 1, m)
            for k in range(KT):
                copy_hT_hi(0, k, attnT_bank[k])

            def gate_silu(b, j, q, reuse=False):
                n = b * IT + j * 2 + q
                act.wait_ge(gate_filled, n + 1)
                nc.scalar.activation(silu[:, q, :], gu_bank[q][0][:], ACT.Silu, scale=col(scales, j * 2 + q)
                                     ).then_inc(silu_done, 1)
                act.wait_ge(fused_done, n + 1)
                if reuse:
                    act.wait_ge(f_free, 1)
                nc.scalar.activation(f_hi[:, q, :], fused[:, q, :], ACT.Copy).then_inc(f_hi_done, 1)

            for n in range(8):
                gate_silu(0, n // 2, n % 2)
                if n in (1, 2, 3):
                    shift_weights(NB, n - 1)
                if n == 3:
                    layernorm(1, 1)
                if n in (4, 5, 6):
                    shift_weights(NB + 1, n - 4)
            with act.Fori(4, NJ) as j:
                for q in range(2):
                    gate_silu(0, j, q)
            for k in range(KT):
                copy_hT_hi(1, k, gu_bank[k // 2][k % 2])
            with act.Fori(1, NB - 1) as b:
                for q in range(2):
                    gate_silu(b, 0, q)
                layernorm(b + 1, 1)
                with act.Fori(1, NJ) as j:
                    for q in range(2):
                        gate_silu(b, j, q)
                for k in range(KT):
                    copy_hT_hi(b + 1, k, gu_bank[k // 2][k % 2])
            with act.Fori(0, NJ - 1) as j:
                for q in range(2):
                    gate_silu(NB - 1, j, q)
            gate_silu(NB - 1, NJ - 1, 0)
            gate_silu(NB - 1, NJ - 1, 1, True)

        @block.tensor
        def _(pe):
            mm = nc.tensor.matmul

            def transpose_ctx(b):
                pe.wait_ge(ctx_here, b + 1)
                for k in range(CT):
                    for n in range(NT):
                        t = nc.tensor.transpose(c_bank[k][:, n * P:(n + 1) * P],
                                                ctx_in[:, n, k * P:(k + 1) * P], ident[:])
                    t.then_inc(ctxT_filled, 1)

            def project(b):
                for i in range(2):
                    for k in range(CT):
                        if i == 0:
                            pe.wait_ge(ctxT_done, b * CT + (k + 1))
                        t = mm(c_bank[i][:], wT[:, i * CT + k, :], ctxT[:, k, :],
                               start=(k == 0), stop=(k == CT - 1))
                    t.then_inc(qk_filled, 1)

            def energies(b, n):
                if n == 0:
                    pe.wait_ge(qk_done, b * 2 + 2)
                if n >= 2:
                    pe.wait_ge(exp_done, b * NT + (n - 1))
                mm(e_bank[n % 2][:], qT[:, n * P:(n + 1) * P], kT[:], start=True, stop=True
                   ).then_inc(energy_filled, 1)

            def transpose_rows(s, k, dst):
                for l in range(LT):
                    t = nc.tensor.transpose(dst[:, l * P:(l + 1) * P], norm[:, l, k * P:(k + 1) * P], ident[:])
                t.then_inc(normT_filled, 1)

            def transpose_x(b, first):
                pe.wait_ge(norm_done, b * LT + LT)
                for k in range(KT):
                    if k >= 2 and not first:
                        pe.wait_ge(x1_done, b * LT + (k - 3))
                    transpose_rows(b, k, xT_bank[k])

            def transpose_attn(b):
                pe.wait_ge(attn_done, b * NT + NT)
                for k in range(NT):
                    if k >= 2:
                        pe.wait_ge(xT_done, b * KT + (k - 1))
                    for n in range(NT):
                        t = nc.tensor.transpose(attnT_bank[k][:, n * P:(n + 1) * P],
                                                attn[:, n, k * P:(k + 1) * P], ident[:])
                    t.then_inc(attnT_filled, 1)

            def mix(b, l):
                if l == 0:
                    pe.wait_ge(xT_done, b * KT + KT)
                if l >= 2:
                    pe.wait_ge(x1_done, b * LT + (l - 1))
                for k in range(KT):
                    if l == 0:
                        pe.wait_ge(attnT_done, b * NT + (k + 1))
                    t = mm(m_bank[l % 2][:], xT[:, k, l * P:(l + 1) * P], attnT[:, k, :],
                           start=(k == 0), stop=(k == KT - 1))
                t.then_inc(mixed, 1)

            pe.wait_ge(consts_done, 2)
            for _ in range(WARM_UP):
                nc.tensor.transpose(e_bank[1][:, 0:P], ident[:], ident[:])
            pe.wait_ge(w_landed, 32)
            for i in range(2):
                for k in range(CT):
                    at = (i * CT + k) * P
                    t = nc.tensor.transpose(t_bank[0][:, at:at + P], w_in[:, i, k * P:(k + 1) * P], ident[:])
            t.then_inc(wT_filled, 1)
            transpose_ctx(0)
            pe.wait_ge(wT_done, 1)
            project(0)
            energies(0, 0)
            energies(0, 1)
            pe.wait_ge(small_landed, 64)
            nc.tensor.transpose(t_bank[1][:, 0:2 * IT], scales_in[:], ident[0:2 * IT, 0:2 * IT]
                                ).then_inc(scalesT_filled, 1)
            transpose_ctx(1)
            energies(0, 2)
            energies(0, 3)
            pe.wait_ge(scales_done, 1)

            def attention(b, first):
                if not first:
                    transpose_ctx(b + 1)
                transpose_x(b, first)
                project(b + 1)
                transpose_attn(b)
                mix(b, 0)
                energies(b + 1, 0)
                energies(b + 1, 1)
                mix(b, 1)
                energies(b + 1, 2)
                energies(b + 1, 3)
                mix(b, 2)
                mix(b, 3)

            attention(0, True)
            with pe.Fori(1, NB - 1) as b:
                attention(b, False)
            transpose_x(NB - 1, False)
            transpose_attn(NB - 1)
            mix(NB - 1, 0)
            mix(NB - 1, 1)
            pe.wait_ge(norm_done, NB * LT + LT)
            for k in range(KT):
                transpose_rows(NB, k, attnT_bank[k])
            mix(NB - 1, 2)
            mix(NB - 1, 3)

            def gate_up(b, j, q, free):
                first = free is None and q == 0
                if free is not None:
                    pe.wait_ge(fused_done, free)
                for w, dst, filled in ((gate_q, gu_bank[q][0], gate_filled), (up_q, gu_bank[q][1], up_filled)):
                    for k in range(KT):
                        if first and w is gate_q:
                            pe.wait_ge(hT_lo_done, b * KT + (k + 1))
                        lhsT = w[:, bass.ds(j, 1), k, q * P:(q + 1) * P].rearrange("p a c -> p (a c)")
                        mm(dst[:], lhsT, hT_hi[:, k, :], start=(k == 0), stop=False)
                        t = mm(dst[:], lhsT, hT_lo[:, k, :], start=False, stop=(k == KT - 1))
                    t.then_inc(filled, 1)

            def down(b, j, q):
                n = b * IT + j * 2 + q
                pe.wait_ge(f_lo_done, n + 1)
                start = isinstance(j, int) and j == 0 and q == 0
                stop = isinstance(j, int) and j == NJ - 1 and q == 1
                rhs = down_q[:, bass.ds(j, 1), q, :].rearrange("p a c -> p (a c)")
                for l in range(LT):
                    mm(acc_bank[l][:], f_hi[:, q, l * P:(l + 1) * P], rhs, start=start, stop=False)
                    t = mm(acc_bank[l][:], f_lo[:, q, l * P:(l + 1) * P], rhs, start=False, stop=stop)
                    if stop:
                        t.then_inc(acc_done, 1)
                if isinstance(b, int) and b == NB - 1 and isinstance(j, int) and j == NJ - 2:
                    t.then_inc(f_free, 1)

            def ffn(b, nexth):
                if isinstance(b, int) and b == 0:
                    pe.wait_ge(weights_done, 3)
                gate_up(b, 0, 0, None)
                gate_up(b, 0, 1, None)
                if isinstance(b, int) and b == 0:
                    pe.wait_ge(x1_done, NB * LT)
                else:
                    pe.wait_ge(y_done, b * LT)
                down(b, 0, 0)
                with pe.Fori(1, NJ if nexth else NJ - 1) as j:
                    pe.wait_ge(weights_done, j * 3 + 3)
                    n = b * IT + j * 2
                    gate_up(b, j, 0, n - 1)
                    down(b, j - 1, 1)
                    gate_up(b, j, 1, n)
                    down(b, j, 0)
                if not nexth:
                    n = b * IT + (NJ - 1) * 2
                    gate_up(b, NJ - 1, 0, n - 1)
                    gate_up(b, NJ - 1, 1, n)
                    down(b, NJ - 2, 1)
                    down(b, NJ - 1, 0)
                if nexth:
                    pe.wait_ge(norm_done, b * LT + (NB * LT + 2 * LT))
                    for k in range(KT):
                        if k % 2 == 0:
                            pe.wait_ge(fused_done, b * IT + (IT - 1 + k // 2))
                        transpose_rows(0, k, gu_bank[k // 2][k % 2])
                down(b, NJ - 1, 1)

            ffn(0, True)
            with pe.Fori(1, NB - 1) as b:
                ffn(b, True)
            ffn(NB - 1, False)


_INPUTS = {
    "x": "x", "ctx_tokens": "ctx_1024", "wq": "L0_xattn_Wq", "bq": "L0_xattn_bq", "wk": "L0_xattn_Wk",
    "bk": "L0_xattn_bk", "gate_w": "L0_ffn_gate_w", "up_w": "L0_ffn_up_w", "down_w": "L0_ffn_down_w",
    "gate_scale": "L0_ffn_gate_scale", "up_scale": "L0_ffn_up_scale", "down_scale": "L0_ffn_down_scale",
}


def kernel(**inputs):
    import numpy as np
    import concourse.bacc as bacc
    from concourse.bass_utils import run_bass_kernel_spmd

    nc = bacc.Bacc("TRN2", target_bir_lowering=False, num_devices=1)
    arrays, aps = {}, {}
    for name, key in _INPUTS.items():
        a = np.ascontiguousarray(inputs[key])
        arrays[f"in_{name}"] = a
        aps[name] = nc.dram_tensor(f"in_{name}", a.shape, mybir.dt.from_np(a.dtype), kind="ExternalInput").ap()
    out = nc.dram_tensor("out_x", arrays["in_x"].shape, F32, kind="ExternalOutput").ap()
    build_xattn_ffn(nc, out=out, **aps)
    result = run_bass_kernel_spmd(nc, [arrays], core_ids=[0])
    return result.results[0]["out_x"]
```

```python
from contextlib import ExitStack

import concourse.bass as bass
from concourse import mybir

F32 = mybir.dt.float32
F32R = mybir.dt.float32r
F16 = mybir.dt.float16
BF16 = mybir.dt.bfloat16
I32 = mybir.dt.int32
ALU = mybir.AluOpType
ACT = mybir.ActivationFunctionType
AX_X = mybir.AxisListType.X

P = 128
WARM_UP = 16
LN_EPS = 1e-5
H_SCALE = 2.0 ** 11
W_SHIFT = 2.0 ** -20
EXPONENT_BITS = 0x7F800000
HALF_BIT = 0x00400000
OVERFLOW_SCALE = 2.0 ** 64 / (464 * W_SHIFT)
FLOOR = 1.5 * 2.0 ** -6


def build_xattn_ffn(nc, x, ctx_tokens, wq, bq, wk, bk, gate_w, up_w, down_w,
                    gate_scale, up_scale, down_scale, out):
    NB, L, H = x.shape
    N, C = ctx_tokens.shape[1:]
    D = wq.shape[0]
    I = gate_w.shape[1]
    LT, KT, NT, CT, IT = L // P, H // P, N // P, C // P, I // P
    NJ = IT // 2
    assert D == P and N == H and L == 512 and H == 512 and LT == KT == NT == 4 and CT == 2
    assert IT % 2 == 0 and NB + 2 == NJ

    x_rows = x.rearrange("b (l p) h -> b p l h", p=P)
    out_rows = out.rearrange("b (l p) h -> b p l h", p=P)
    ctx_rows = ctx_tokens.rearrange("b (n p) c -> b p n c", p=P)
    gate_cols = gate_w.rearrange("(k p) (j c) -> j p k c", p=P, c=2 * P)
    up_cols = up_w.rearrange("(k p) (j c) -> j p k c", p=P, c=2 * P)
    down_rows = down_w.rearrange("(j t p) h -> j p t h", p=P, t=2)

    with ExitStack() as stack:
        def sb(name, shape, dt):
            return stack.enter_context(nc.sbuf_tensor(name, shape, dt))

        def sem(name):
            return stack.enter_context(nc.semaphore(name))

        x_all = sb("x_all", [P, NB * LT, H], F32)
        ctx_in = sb("ctx_in", [P, NT, C], F32)
        wT = sb("wT", [P, 2 * CT, D], F32)
        bias = sb("bias", [P, 2], F32)
        ident = sb("ident", [P, P], F32)
        norm = sb("norm", [P, LT, H], F32)
        xT = sb("xT", [P, KT, L], F32)
        ctxT = sb("ctxT", [P, CT, N], F32)
        qT = sb("qT", [P, N], F32)
        kT = sb("kT", [P, N], F32)
        attn = sb("attn", [P, NT, H], F32)
        w_in = attn[:, 0, :].rearrange("p (i c) -> p i c", i=2)
        attnT = sb("attnT", [P, NT, H], F32)
        part = sb("part", [P, 2 * LT, 6], F32)
        meanvar = sb("meanvar", [P, 2 * LT, 2], F32)
        ln_var = sb("ln_var", [P, 2, LT], F32)
        ln_mean = sb("ln_mean", [P, 2, LT], F32)
        ln_scale = sb("ln_scale", [P, 2 * NB, LT], F32)
        ln_shift = sb("ln_shift", [P, 2 * NB, LT], F32)
        minus_half = sb("minus_half", [P, LT], F32)
        neg_max = sb("neg_max", [P, NB * NT], F32)
        exp_sum = sb("exp_sum", [P, NB * NT], F32)
        inv_sum = sb("inv_sum", [P, NB * NT], F32)
        raw = sb("raw", [P, 2 * 3, 1024], F32)
        magic = sb("magic", [P, 3, 1024], F32)
        gate_q = sb("gate_q", [P, NJ, KT, 2 * P], BF16)
        up_q = sb("up_q", [P, NJ, KT, 2 * P], BF16)
        down_q = sb("down_q", [P, NJ, 2, H], F32R)
        scales_in = sb("scales_in", [2 * IT, P], F32)
        scales = sb("scales", [P, 2 * IT], F32)
        down_s = sb("down_s", [P, H], F32)
        hT_hi = sb("hT_hi", [P, KT, L], F16)
        hT_lo = sb("hT_lo", [P, KT, L], F16)
        silu = sb("silu", [P, 2, L], F32)
        fused = sb("fused", [P, 2, L], F32)
        f_hi = sb("f_hi", [P, 2, L], F32R)
        f_lo = sb("f_lo", [P, 2, L], F32R)
        last_hi = sb("last_hi", [P, L], F32R)
        last_lo = sb("last_lo", [P, L], F32R)
        y = sb("y", [P, LT, H], F32)
        flaw = y[:, :, :].rearrange("p l h -> p (l h)").rearrange("p (a n) -> p a n", a=2)

        bank = [stack.enter_context(nc.psum_tensor(f"bank{i}", [P, 512], F32)) for i in range(8)]
        t_bank, m_bank, e_bank, c_bank = bank[0:2], bank[2:4], bank[4:6], bank[6:8]
        xT_bank = bank[0:4]
        attnT_bank = bank[4:6] + bank[0:2]
        acc_bank = bank[0:4]
        gu_bank = [bank[4:6], bank[6:8]]

        w_landed = sem("w_landed")
        small_landed = sem("small_landed")
        down_s_landed = sem("down_s_landed")
        x_landed = [sem(f"x_landed{b}") for b in range(NB)]
        ctx_landed = [sem(f"ctx_landed{b}") for b in range(NB)]
        raw_landed = [sem(f"raw_landed{j}") for j in range(NJ)]
        x_here = sem("x_here")
        ctx_here = sem("ctx_here")
        raw_here = sem("raw_here")
        consts_step = sem("consts_step")
        consts_done = sem("consts_done")
        down_s_done = sem("down_s_done")
        wT_filled, wT_done = sem("wT_filled"), sem("wT_done")
        scalesT_filled, scales_done = sem("scalesT_filled"), sem("scales_done")
        x_part, x_stats = sem("x_part"), sem("x_stats")
        h_part, h_stats = sem("h_part"), sem("h_stats")
        moments = [sem("x_moments"), sem("h_moments")]
        ln_step = [sem("x_ln_step"), sem("h_ln_step")]
        ln_done = [sem("x_ln_done"), sem("h_ln_done")]
        norm_done = sem("norm_done")
        normT_filled = sem("normT_filled")
        xT_done = sem("xT_done")
        ctxT_filled, ctxT_done = sem("ctxT_filled"), sem("ctxT_done")
        qk_filled, qk_done = sem("qk_filled"), sem("qk_done")
        energy_filled = sem("energy_filled")
        max_done, exp_done = sem("max_done"), sem("exp_done")
        inv_done, attn_done = sem("inv_done"), sem("attn_done")
        attnT_filled = sem("attnT_filled")
        attnT_done = sem("attnT_done")
        mixed = sem("mixed")
        x1_done = sem("x1_done")
        magic_done, shifted, summed = sem("magic_done"), sem("shifted"), sem("summed")
        weights_done = sem("weights_done")
        squared = sem("squared")
        flaw_clear = sem("flaw_clear")
        tested = sem("tested")
        fold_step, flaws_done = sem("fold_step"), sem("flaws_done")
        hT_hi_done, hT_lo_done = sem("hT_hi_done"), sem("hT_lo_done")
        gate_filled, up_filled = sem("gate_filled"), sem("up_filled")
        silu_done, fused_done = sem("silu_done"), sem("fused_done")
        f_hi_done, f_lo_done = sem("f_hi_done"), sem("f_lo_done")
        acc_done = sem("acc_done")
        y_done, out_done = sem("y_done"), sem("out_done")
        odd_y_done = sem("odd_y_done")
        odd_out_done = sem("odd_out_done")
        out_landed = sem("out_landed")

        def row(buf, i):
            return buf[:, bass.ds(i, 1), :].rearrange("p a n -> p (a n)")

        def col(buf, i):
            return buf[:, bass.ds(i, 1)]

        block = stack.enter_context(nc.Block())

        @block.sync
        def _(sp):
            raw_src = [gate_cols, up_cols, down_rows]

            def load_weights(j):
                for m in range(3):
                    dst = raw[:, (j % 2) * 3 + m, :].rearrange("p (k c) -> p k c", k=raw_src[m].shape[2])
                    sp.dma_start(dst, raw_src[m][j]).then_inc(raw_landed[j], 16)

            def load_x(b):
                sp.dma_start(x_all[:, b * LT:(b + 1) * LT, :], x_rows[b]).then_inc(x_landed[b], 16)

            def load_ctx(b):
                sp.dma_start(ctx_in[:], ctx_rows[b]).then_inc(ctx_landed[b], 16)

            def pass_on(landed, value, here):
                sp.wait_ge(landed, value)
                sp.sem_inc(here, 1)

            sp.dma_start(w_in[:, 0, :], wq).then_inc(w_landed, 16)
            sp.dma_start(w_in[:, 1, :], wk).then_inc(w_landed, 16)
            load_ctx(0)
            load_x(0)
            sp.dma_start(bias[:, 0:1], bq.rearrange("(p a) -> p a", a=1)).then_inc(small_landed, 16)
            sp.dma_start(bias[:, 1:2], bk.rearrange("(p a) -> p a", a=1)).then_inc(small_landed, 16)
            sp.dma_start(scales_in[0:IT, :], gate_scale.rearrange("(i p) -> i p", p=P)).then_inc(small_landed, 16)
            sp.dma_start(scales_in[IT:2 * IT, :], up_scale.rearrange("(i p) -> i p", p=P)
                         ).then_inc(small_landed, 16)
            pass_on(ctx_landed[0], 16, ctx_here)
            sp.wait_ge(ctxT_filled, CT)
            load_ctx(1)
            load_weights(0)
            load_x(1)
            load_weights(1)
            sp.dma_start(down_s[:], down_scale.rearrange("(a h) -> a h", a=1).broadcast_to([P, H])
                         ).then_inc(down_s_landed, 16)
            pass_on(x_landed[0], 16, x_here)
            pass_on(ctx_landed[1], 16, ctx_here)
            pass_on(raw_landed[0], 48, raw_here)
            pass_on(x_landed[1], 16, x_here)
            for b in range(2, NB):
                sp.wait_ge(ctxT_filled, CT * b)
                load_ctx(b)
                load_x(b)
                pass_on(raw_landed[b - 1], 48, raw_here)
                pass_on(ctx_landed[b], 16, ctx_here)
                pass_on(x_landed[b], 16, x_here)
                sp.wait_ge(tested, 3 * (b - 1))
                load_weights(b)
            for j in range(NB, NJ):
                pass_on(raw_landed[j - 1], 48, raw_here)
                sp.wait_ge(tested, 3 * (j - 1))
                load_weights(j)
            pass_on(raw_landed[NJ - 1], 48, raw_here)
            with sp.Fori(0, NB - 1) as b:
                for l in range(LT):
                    sp.wait_ge(out_done, b * LT + (l + 1))
                    sp.dma_start(out_rows[bass.ds(b, 1), :, l, :].rearrange("a p h -> (a p) h"), y[:, l, :]
                                 ).then_inc(out_landed, 16)
            for l in range(LT):
                if l % 2 == 0:
                    sp.wait_ge(out_done, (NB - 1) * LT + (l // 2 + 1))
                else:
                    sp.wait_ge(odd_out_done, l // 2 + 1)
                sp.dma_start(out_rows[NB - 1, :, l, :], y[:, l, :]).then_inc(out_landed, 16)
            sp.wait_ge(out_landed, 16 * NB * LT)

        @block.gpsimd
        def _(pool):
            nc.gpsimd.memset(ident[:], 0.0).then_inc(consts_step, 1)
            pool.wait_ge(consts_step, 1)
            nc.gpsimd.affine_select(out=ident[:], in_=ident[:], compare_op=ALU.not_equal, fill=1.0, base=0,
                                    pattern=[[-1, P]], channel_multiplier=1).then_inc(consts_done, 1)
            nc.gpsimd.memset(minus_half[:], -0.5).then_inc(consts_done, 1)
            pool.wait_ge(consts_done, 2)
            pool.sem_inc(ln_done[1], 1)

            def ln_factors(b, kind):
                s = b + kind * NB
                pool.wait_ge(moments[kind], b * 2 + 2)
                nc.gpsimd.tensor_tensor(row(ln_scale, s), ln_var[:, kind, :], minus_half[:], ALU.pow
                                        ).then_inc(ln_step[kind], 1)
                pool.wait_ge(ln_step[kind], b + 1)
                nc.gpsimd.tensor_tensor(row(ln_shift, s), ln_mean[:, kind, :], row(ln_scale, s), ALU.mult
                                        ).then_inc(ln_done[kind], 1)

            nc.gpsimd.memset(y[:], 0.0).then_inc(flaw_clear, 1)

            def test_weights(j, ms=range(3)):
                for m in ms:
                    pool.wait_ge(squared, j * 3 + (m + 1))
                    if isinstance(j, int) and j == 0 and m == 0:
                        pool.wait_ge(flaw_clear, 1)
                    else:
                        pool.wait_ge(tested, j * 3 + m)
                    acc = flaw[:, m // 2, :]
                    nc.gpsimd.tensor_tensor(acc, acc, row(raw, (j % 2) * 3 + m), ALU.mult).then_inc(tested, 1)

            def mark_flaws():
                pool.wait_ge(tested, 3 * NJ)
                steps, width = 0, flaw.shape[2]
                while width > 1:
                    width //= 2
                    if steps:
                        pool.wait_ge(fold_step, steps)
                    nc.gpsimd.tensor_tensor(flaw[:, 0, 0:width], flaw[:, 0, 0:width],
                                            flaw[:, 0, width:2 * width], ALU.add).then_inc(fold_step, 1)
                    steps += 1
                last_row = down_q[:, NJ - 1, 1, :]
                nc.gpsimd.tensor_tensor(flaw[:, 1, 0:H], flaw[:, 1, 0:H], flaw[:, 1, H:2 * H], ALU.add
                                        ).then_inc(fold_step, 1)
                pool.wait_ge(fold_step, steps + 1)
                nc.gpsimd.tensor_scalar(flaw[:, 1, 0:H], flaw[:, 1, 0:H], flaw[:, 0, 0:1], None, ALU.add
                                        ).then_inc(fold_step, 1)
                pool.wait_ge(fold_step, steps + 2)
                nc.gpsimd.tensor_tensor(last_row, flaw[:, 1, 0:H], last_row.bitcast(F32), ALU.add
                                        ).then_inc(flaws_done, 1)

            ln_factors(0, 0)
            ln_factors(1, 0)
            test_weights(0, (0, 1))
            with pool.Fori(1, NB - 1) as b:
                ln_factors(b - 1, 1)
                ln_factors(b + 1, 0)
                test_weights(b - 1, (2,))
                test_weights(b, (0, 1))
            ln_factors(NB - 2, 1)
            test_weights(NB - 2, (2,))
            ln_factors(NB - 1, 1)
            with pool.Fori(NB - 1, NJ) as j:
                test_weights(j)
            mark_flaws()

            def add_residual(b):
                for l in range(LT):
                    pool.wait_ge(y_done, b * LT + (l + 1))
                    nc.gpsimd.tensor_tensor(y[:, l, :], y[:, l, :], row(x_all, b * LT + l), ALU.add
                                            ).then_inc(out_done, 1)

            with pool.Fori(0, NB - 1) as b:
                add_residual(b)
            for i in range(LT // 2):
                pool.wait_ge(y_done, (NB - 1) * LT + (i + 1))
                nc.gpsimd.tensor_tensor(y[:, 2 * i, :], y[:, 2 * i, :], x_all[:, (NB - 1) * LT + 2 * i, :], ALU.add
                                        ).then_inc(out_done, 1)

        @block.vector
        def _(dve):
            def x_parts(b):
                for l in range(LT):
                    nc.vector.bn_stats(part[:, l, :], row(x_all, b * LT + l)).then_inc(x_part, 1)

            def h_parts(b, l):
                nc.vector.bn_stats(part[:, LT + l, :], row(x_all, b * LT + l)).then_inc(h_part, 1)

            def statistics(b, kind):
                stats = [x_stats, h_stats][kind]
                for l in range(LT):
                    nc.vector.bn_aggr(meanvar[:, kind * LT + l, :], part[:, kind * LT + l, :]).then_inc(stats, 1)
                if kind or not isinstance(b, int) or b:
                    dve.wait_ge(ln_done[kind], b + kind)
                dve.wait_ge(stats, b * LT + LT)
                mv = meanvar[:, kind * LT:(kind + 1) * LT, :]
                nc.vector.tensor_scalar(ln_var[:, kind, :], mv[:, :, 1], LN_EPS, H_SCALE ** -2, ALU.add, ALU.mult
                                        ).then_inc(moments[kind], 1)
                nc.vector.tensor_scalar_mul(ln_mean[:, kind, :], mv[:, :, 0], -1.0).then_inc(moments[kind], 1)

            def magic_numbers(j, ms=range(3)):
                for m in ms:
                    if m == 0:
                        if not isinstance(j, int) or j:
                            dve.wait_ge(weights_done, j * 3)
                        dve.wait_ge(raw_here, j + 1)
                    nc.vector.tensor_scalar(magic[:, m, :].bitcast(I32), row(raw, (j % 2) * 3 + m).bitcast(I32),
                                            EXPONENT_BITS, HALF_BIT, ALU.bitwise_and, ALU.bitwise_or
                                            ).then_inc(magic_done, 1)

            def round_weights(j, m):
                w = row(raw, (j % 2) * 3 + m)
                dve.wait_ge(shifted, j * 3 + (m + 1))
                nc.vector.scalar_tensor_tensor(w, magic[:, m, :], FLOOR, w, ALU.max, ALU.add).then_inc(summed, 1)
                dst = [gate_q, up_q, down_q][m][:, bass.ds(j, 1), :, :].rearrange("p a k c -> p (a k c)")
                dve.wait_ge(summed, j * 3 + (m + 1))
                nc.vector.scalar_tensor_tensor(dst, magic[:, m, :], FLOOR, w, ALU.max, ALU.subtract
                                               ).then_inc(weights_done, 1)

            def energy_max(b, n):
                dve.wait_ge(energy_filled, b * NT + (n + 1))
                nc.vector.reduce_max(col(neg_max, b * NT + n), e_bank[n % 2][:], axis=AX_X, negate=True
                                     ).then_inc(max_done, 1)

            def invert_sum(b, n):
                dve.wait_ge(exp_done, b * NT + (n + 1))
                nc.vector.reciprocal(col(inv_sum, b * NT + n), col(exp_sum, b * NT + n)).then_inc(inv_done, 1)

            def x1_rows(b, l):
                dve.wait_ge(mixed, b * LT + (l + 1))
                xr = row(x_all, b * LT + l)
                nc.vector.scalar_tensor_tensor(xr, m_bank[l % 2][:], 1.0 / H_SCALE, xr, ALU.mult, ALU.add
                                               ).then_inc(x1_done, 1)

            dve.wait_ge(wT_filled, 1)
            nc.vector.tensor_copy(wT[:, :, :].rearrange("p t d -> p (t d)"), t_bank[0][:]).then_inc(wT_done, 1)
            dve.wait_ge(x_landed[0], 16)
            x_parts(0)
            dve.wait_ge(x_part, LT)
            statistics(0, 0)
            energy_max(0, 0)
            energy_max(0, 1)
            dve.wait_ge(scalesT_filled, 1)
            nc.vector.tensor_scalar_mul(scales[:], t_bank[1][:, 0:2 * IT], -1.0 / (W_SHIFT * H_SCALE)
                                        ).then_inc(scales_done, 1)
            invert_sum(0, 0)
            dve.wait_ge(ln_done[0], 1)
            for l in range(LT):
                nc.vector.tensor_scalar(norm[:, l, :], x_all[:, l, :], ln_scale[:, 0, l:l + 1],
                                        ln_shift[:, 0, l:l + 1], ALU.mult, ALU.add).then_inc(norm_done, 1)
            invert_sum(0, 1)
            energy_max(0, 2)
            energy_max(0, 3)
            invert_sum(0, 2)
            invert_sum(0, 3)

            def attention(b, first):
                if not first:
                    x1_rows(b - 1, 3)
                    dve.wait_ge(x1_done, b * LT)
                dve.wait_ge(x_here, b + 2)
                magic_numbers(b, (0,))
                if not first:
                    h_parts(b - 1, 3)
                    dve.wait_ge(h_part, b * LT)
                magic_numbers(b, (1,))
                if not first:
                    statistics(b - 1, 1)
                x_parts(b + 1)
                dve.wait_ge(x_part, b * LT + 2 * LT)
                magic_numbers(b, (2,))
                statistics(b + 1, 0)
                round_weights(b, 0)
                if not first:
                    round_weights(b, 1)
                x1_rows(b, 0)
                dve.wait_ge(x1_done, b * LT + 1)
                energy_max(b + 1, 0)
                energy_max(b + 1, 1)
                invert_sum(b + 1, 0)
                h_parts(b, 0)
                invert_sum(b + 1, 1)
                if first:
                    round_weights(b, 1)
                x1_rows(b, 1)
                dve.wait_ge(x1_done, b * LT + 2)
                energy_max(b + 1, 2)
                energy_max(b + 1, 3)
                invert_sum(b + 1, 2)
                h_parts(b, 1)
                invert_sum(b + 1, 3)
                x1_rows(b, 2)
                dve.wait_ge(x1_done, b * LT + 3)
                round_weights(b, 2)
                h_parts(b, 2)

            attention(0, True)
            with dve.Fori(1, NB - 1) as b:
                attention(b, False)

            def copy_hT_lo(b, k, src):
                dve.wait_ge(hT_hi_done, b * KT + (k + 1))
                nc.vector.tensor_tensor(hT_lo[:, k, :], src[:], hT_hi[:, k, :], ALU.subtract
                                        ).then_inc(hT_lo_done, 1)

            last = NB - 1
            x1_rows(last - 1, 3)
            magic_numbers(last)
            dve.wait_ge(x1_done, last * LT)
            h_parts(last - 1, 3)
            dve.wait_ge(h_part, last * LT)
            statistics(last - 1, 1)
            round_weights(last, 0)
            for l in range(LT):
                x1_rows(last, l)
                dve.wait_ge(x1_done, last * LT + (l + 1))
                h_parts(last, l)
                if l == 1:
                    for k in range(KT):
                        copy_hT_lo(0, k, attnT_bank[k])
                if l < 2:
                    round_weights(last, 1 + l)
            dve.wait_ge(h_part, NB * LT)
            statistics(last, 1)
            dve.wait_ge(down_s_landed, 16)
            nc.vector.tensor_scalar_mul(down_s[:], down_s[:], -1.0 / W_SHIFT).then_inc(down_s_done, 1)

            def fuse(b, j, q, hi=None, lo=None):
                n = b * IT + j * 2 + q
                dve.wait_ge(silu_done, n + 1)
                dve.wait_ge(up_filled, n + 1)
                nc.vector.scalar_tensor_tensor(fused[:, q, :], gu_bank[q][1][:], col(scales, j * 2 + (IT + q)),
                                               silu[:, q, :], ALU.mult, ALU.mult).then_inc(fused_done, 1)
                dve.wait_ge(f_hi_done, n + 1)
                nc.vector.tensor_tensor(f_lo[:, q, :] if lo is None else lo[:], fused[:, q, :],
                                        (f_hi[:, q, :] if hi is None else hi[:]).bitcast(F32), ALU.subtract
                                        ).then_inc(f_lo_done, 1)

            def scale_output(b, first):
                if first:
                    dve.wait_ge(down_s_done, 1)
                if not first:
                    dve.wait_ge(out_landed, b * (16 * LT))
                for l in range(LT):
                    dve.wait_ge(acc_done, b * LT + (l + 1))
                    nc.vector.tensor_tensor(y[:, l, :], acc_bank[l][:], down_s[:], ALU.mult).then_inc(y_done, 1)

            for n in range(8):
                fuse(0, n // 2, n % 2)
                if n in (0, 4):
                    magic_numbers(NB + n // 4)
                else:
                    round_weights(NB + n // 4, n % 4 - 1)
            with dve.Fori(4, NJ) as j:
                for q in range(2):
                    fuse(0, j, q)
            for k in range(KT):
                copy_hT_lo(1, k, gu_bank[k // 2][k % 2])
            scale_output(0, True)
            with dve.Fori(1, NB - 1) as b:
                with dve.Fori(0, NJ) as j:
                    for q in range(2):
                        fuse(b, j, q)
                for k in range(KT):
                    copy_hT_lo(b + 1, k, gu_bank[k // 2][k % 2])
                scale_output(b, False)
            with dve.Fori(0, NJ - 1) as j:
                for q in range(2):
                    fuse(last, j, q)
            fuse(last, NJ - 1, 0)
            fuse(last, NJ - 1, 1, last_hi, last_lo)
            dve.wait_ge(out_landed, last * (16 * LT))

            def scale_last(l):
                dve.wait_ge(acc_done, last * LT + (l + 1))
                nc.vector.tensor_tensor(y[:, l, :], acc_bank[l][:], down_s[:], ALU.mult
                                        ).then_inc([y_done, odd_y_done][l % 2], 1)

            def add_residual(l):
                dve.wait_ge(odd_y_done, l // 2 + 1)
                nc.vector.tensor_tensor(y[:, l, :], y[:, l, :], x_all[:, last * LT + l, :], ALU.add
                                        ).then_inc(odd_out_done, 1)

            scale_last(0)
            scale_last(1)
            scale_last(2)
            add_residual(1)
            scale_last(3)
            add_residual(3)

        @block.scalar
        def _(act):
            def shift_weights(j, m):
                act.wait_ge(magic_done, j * 3 + (m + 1))
                w = row(raw, (j % 2) * 3 + m)
                nc.scalar.activation(w, w, ACT.Copy, scale=W_SHIFT).then_inc(shifted, 1)

            def square_weights(j, m):
                act.wait_ge(weights_done, j * 3 + (m + 1))
                q = [gate_q, up_q, down_q][m][:, bass.ds(j, 1), :, :].rearrange("p a k c -> p (a k c)")
                nc.scalar.activation(row(raw, (j % 2) * 3 + m), q.bitcast(F32) if m == 2 else q, ACT.Square,
                                     scale=OVERFLOW_SCALE).then_inc(squared, 1)

            def copy_xT(b, k):
                act.wait_ge(normT_filled, b * KT + (k + 1))
                nc.scalar.activation(xT[:, k, :], xT_bank[k][:], ACT.Copy).then_inc(xT_done, 1)

            def copy_attnT(b, k):
                act.wait_ge(attnT_filled, b * NT + (k + 1))
                nc.scalar.activation(attnT[:, k, :], attnT_bank[k][:], ACT.Copy).then_inc(attnT_done, 1)

            def copy_ctxT(b):
                for k in range(CT):
                    act.wait_ge(ctxT_filled, b * CT + (k + 1))
                    nc.scalar.activation(ctxT[:, k, :], c_bank[k][:], ACT.Copy).then_inc(ctxT_done, 1)

            def copy_qk(b, i):
                act.wait_ge(qk_filled, b * 2 + (i + 1))
                nc.scalar.activation([qT, kT][i][:], c_bank[i][:], ACT.Identity, bias=bias[:, i:i + 1]
                                     ).then_inc(qk_done, 1)

            def exponentials(b, n):
                act.wait_ge(max_done, b * NT + (n + 1))
                nc.scalar.activation(attn[:, n, :], e_bank[n % 2][:], ACT.Exp,
                                     bias=col(neg_max, b * NT + n), accum_out=col(exp_sum, b * NT + n)
                                     ).then_inc(exp_done, 1)

            def normalise(b, n):
                act.wait_ge(inv_done, b * NT + (n + 1))
                nc.scalar.activation(attn[:, n, :], attn[:, n, :], ACT.Copy, scale=col(inv_sum, b * NT + n)
                                     ).then_inc(attn_done, 1)

            def softmax(b, n0):
                exponentials(b, n0)
                exponentials(b, n0 + 1)
                normalise(b, n0)
                normalise(b, n0 + 1)

            def layernorm(b, kind):
                s = b + kind * NB
                act.wait_ge(ln_done[kind], b + (1 + kind))
                act.wait_ge(normT_filled, s * KT)
                for l in range(LT):
                    nc.scalar.activation(norm[:, l, :], row(x_all, b * LT + l), ACT.Identity,
                                         bias=ln_shift[:, bass.ds(s, 1), l:l + 1].rearrange("p a n -> p (a n)"),
                                         scale=ln_scale[:, bass.ds(s, 1), l:l + 1].rearrange("p a n -> p (a n)")
                                         ).then_inc(norm_done, 1)

            copy_ctxT(0)
            act.wait_ge(small_landed, 64)
            copy_qk(0, 0)
            copy_qk(0, 1)
            softmax(0, 0)
            copy_ctxT(1)
            softmax(0, 2)

            def attention(b, first):
                if not first:
                    copy_ctxT(b + 1)
                for k in range(KT):
                    copy_xT(b, k)
                if not first:
                    shift_weights(b, 0)
                copy_qk(b + 1, 0)
                if not first:
                    shift_weights(b, 1)
                    copy_qk(b + 1, 1)
                for k in range(NT):
                    copy_attnT(b, k)
                if first:
                    copy_qk(b + 1, 1)
                    shift_weights(b, 0)
                    shift_weights(b, 1)
                else:
                    square_weights(b - 1, 2)
                layernorm(b + 1, 0)
                shift_weights(b, 2)
                softmax(b + 1, 0)
                square_weights(b, 0)
                square_weights(b, 1)
                softmax(b + 1, 2)

            attention(0, True)
            with act.Fori(1, NB - 1) as b:
                attention(b, False)

            def copy_hT_hi(b, k, src):
                act.wait_ge(normT_filled, b * KT + (NB * KT + k + 1))
                nc.scalar.activation(hT_hi[:, k, :], src[:], ACT.Copy).then_inc(hT_hi_done, 1)

            for k in range(KT):
                copy_xT(NB - 1, k)
            for k in range(NT):
                copy_attnT(NB - 1, k)
            shift_weights(NB - 1, 0)
            layernorm(0, 1)
            shift_weights(NB - 1, 1)
            shift_weights(NB - 1, 2)
            for k in range(KT):
                copy_hT_hi(0, k, attnT_bank[k])
            square_weights(NB - 2, 2)
            square_weights(NB - 1, 0)
            square_weights(NB - 1, 1)
            square_weights(NB - 1, 2)
            layernorm(1, 1)

            def gate_silu(b, j, q, hi=None):
                n = b * IT + j * 2 + q
                act.wait_ge(gate_filled, n + 1)
                nc.scalar.activation(silu[:, q, :], gu_bank[q][0][:], ACT.Silu, scale=col(scales, j * 2 + q)
                                     ).then_inc(silu_done, 1)
                act.wait_ge(fused_done, n + 1)
                nc.scalar.activation(f_hi[:, q, :] if hi is None else hi[:], fused[:, q, :], ACT.Copy
                                     ).then_inc(f_hi_done, 1)

            for n in range(8):
                gate_silu(0, n // 2, n % 2)
                if n in (3, 4):
                    square_weights(NB, 2 * (n - 3))
                if n == 3:
                    square_weights(NB, 1)
                if n in (6, 7):
                    square_weights(NB + 1, n - 6)
                if n < 3:
                    shift_weights(NB, n)
                elif n in (4, 5, 6):
                    shift_weights(NB + 1, n - 4)
            square_weights(NB + 1, 2)
            with act.Fori(4, NJ) as j:
                for q in range(2):
                    gate_silu(0, j, q)
            for k in range(KT):
                copy_hT_hi(1, k, gu_bank[k // 2][k % 2])
            with act.Fori(1, NB - 1) as b:
                for q in range(2):
                    gate_silu(b, 0, q)
                layernorm(b + 1, 1)
                with act.Fori(1, NJ) as j:
                    for q in range(2):
                        gate_silu(b, j, q)
                for k in range(KT):
                    copy_hT_hi(b + 1, k, gu_bank[k // 2][k % 2])
            with act.Fori(0, NJ - 1) as j:
                for q in range(2):
                    gate_silu(NB - 1, j, q)
            gate_silu(NB - 1, NJ - 1, 0)
            gate_silu(NB - 1, NJ - 1, 1, last_hi)

        @block.tensor
        def _(pe):
            mm = nc.tensor.matmul

            def transpose_ctx(b):
                pe.wait_ge(ctx_here, b + 1)
                for k in range(CT):
                    for n in range(NT):
                        t = nc.tensor.transpose(c_bank[k][:, n * P:(n + 1) * P],
                                                ctx_in[:, n, k * P:(k + 1) * P], ident[:])
                    t.then_inc(ctxT_filled, 1)

            def project(b):
                for i in range(2):
                    for k in range(CT):
                        if i == 0:
                            pe.wait_ge(ctxT_done, b * CT + (k + 1))
                        t = mm(c_bank[i][:], wT[:, i * CT + k, :], ctxT[:, k, :],
                               start=(k == 0), stop=(k == CT - 1))
                    t.then_inc(qk_filled, 1)

            def energies(b, n):
                if n == 0:
                    pe.wait_ge(qk_done, b * 2 + 2)
                if n >= 2:
                    pe.wait_ge(exp_done, b * NT + (n - 1))
                mm(e_bank[n % 2][:], qT[:, n * P:(n + 1) * P], kT[:], start=True, stop=True
                   ).then_inc(energy_filled, 1)

            def transpose_rows(s, k, dst):
                for l in range(LT):
                    t = nc.tensor.transpose(dst[:, l * P:(l + 1) * P], norm[:, l, k * P:(k + 1) * P], ident[:])
                t.then_inc(normT_filled, 1)

            def transpose_x(b, first):
                pe.wait_ge(norm_done, b * LT + LT)
                for k in range(KT):
                    if k >= 2 and not first:
                        pe.wait_ge(x1_done, b * LT + (k - 3))
                    transpose_rows(b, k, xT_bank[k])

            def transpose_attn(b):
                pe.wait_ge(attn_done, b * NT + NT)
                for k in range(NT):
                    if k >= 2:
                        pe.wait_ge(xT_done, b * KT + (k - 1))
                    for n in range(NT):
                        t = nc.tensor.transpose(attnT_bank[k][:, n * P:(n + 1) * P],
                                                attn[:, n, k * P:(k + 1) * P], ident[:])
                    t.then_inc(attnT_filled, 1)

            def mix(b, l):
                if l == 0:
                    pe.wait_ge(xT_done, b * KT + KT)
                if l >= 2:
                    pe.wait_ge(x1_done, b * LT + (l - 1))
                for k in range(KT):
                    if l == 0:
                        pe.wait_ge(attnT_done, b * NT + (k + 1))
                    t = mm(m_bank[l % 2][:], xT[:, k, l * P:(l + 1) * P], attnT[:, k, :],
                           start=(k == 0), stop=(k == KT - 1))
                t.then_inc(mixed, 1)

            pe.wait_ge(consts_done, 2)
            for _ in range(WARM_UP):
                nc.tensor.transpose(e_bank[1][:, 0:P], ident[:], ident[:])
            pe.wait_ge(w_landed, 32)
            for i in range(2):
                for k in range(CT):
                    at = (i * CT + k) * P
                    t = nc.tensor.transpose(t_bank[0][:, at:at + P], w_in[:, i, k * P:(k + 1) * P], ident[:])
            t.then_inc(wT_filled, 1)
            transpose_ctx(0)
            pe.wait_ge(wT_done, 1)
            project(0)
            energies(0, 0)
            energies(0, 1)
            pe.wait_ge(small_landed, 64)
            nc.tensor.transpose(t_bank[1][:, 0:2 * IT], scales_in[:], ident[0:2 * IT, 0:2 * IT]
                                ).then_inc(scalesT_filled, 1)
            transpose_ctx(1)
            energies(0, 2)
            energies(0, 3)
            pe.wait_ge(scales_done, 1)

            def attention(b, first):
                if not first:
                    transpose_ctx(b + 1)
                transpose_x(b, first)
                project(b + 1)
                transpose_attn(b)
                mix(b, 0)
                energies(b + 1, 0)
                energies(b + 1, 1)
                mix(b, 1)
                energies(b + 1, 2)
                energies(b + 1, 3)
                mix(b, 2)
                mix(b, 3)

            attention(0, True)
            with pe.Fori(1, NB - 1) as b:
                attention(b, False)
            transpose_x(NB - 1, False)
            transpose_attn(NB - 1)
            mix(NB - 1, 0)
            mix(NB - 1, 1)
            pe.wait_ge(norm_done, NB * LT + LT)
            for k in range(KT):
                transpose_rows(NB, k, attnT_bank[k])
            mix(NB - 1, 2)
            mix(NB - 1, 3)

            def gate_up(b, j, q, free):
                first = free is None and q == 0
                if free is not None:
                    pe.wait_ge(fused_done, free)
                for w, dst, filled in ((gate_q, gu_bank[q][0], gate_filled), (up_q, gu_bank[q][1], up_filled)):
                    for k in range(KT):
                        if first and w is gate_q:
                            pe.wait_ge(hT_lo_done, b * KT + (k + 1))
                        lhsT = w[:, bass.ds(j, 1), k, q * P:(q + 1) * P].rearrange("p a c -> p (a c)")
                        mm(dst[:], lhsT, hT_hi[:, k, :], start=(k == 0), stop=False)
                        t = mm(dst[:], lhsT, hT_lo[:, k, :], start=False, stop=(k == KT - 1))
                    t.then_inc(filled, 1)

            def down_rows(l, j, q, hi, lo):
                start = isinstance(j, int) and j == 0 and q == 0
                stop = isinstance(j, int) and j == NJ - 1 and q == 1
                rhs = down_q[:, bass.ds(j, 1), q, :].rearrange("p a c -> p (a c)")
                mm(acc_bank[l][:], hi[:, l * P:(l + 1) * P], rhs, start=start, stop=False)
                t = mm(acc_bank[l][:], lo[:, l * P:(l + 1) * P], rhs, start=False, stop=stop)
                if stop:
                    t.then_inc(acc_done, 1)

            def down(b, j, q):
                pe.wait_ge(f_lo_done, b * IT + j * 2 + (q + 1))
                for l in range(LT):
                    down_rows(l, j, q, f_hi[:, q, :], f_lo[:, q, :])

            def ffn_steps(b, end):
                if isinstance(b, int) and b == 0:
                    pe.wait_ge(weights_done, 3)
                gate_up(b, 0, 0, None)
                gate_up(b, 0, 1, None)
                if isinstance(b, int) and b == 0:
                    pe.wait_ge(x1_done, NB * LT)
                else:
                    pe.wait_ge(y_done, b * LT)
                down(b, 0, 0)
                with pe.Fori(1, end) as j:
                    pe.wait_ge(weights_done, j * 3 + 3)
                    n = b * IT + j * 2
                    gate_up(b, j, 0, n - 1)
                    down(b, j - 1, 1)
                    gate_up(b, j, 1, n)
                    down(b, j, 0)

            def ffn(b):
                ffn_steps(b, NJ)
                pe.wait_ge(norm_done, b * LT + (NB * LT + 2 * LT))
                for k in range(KT):
                    if k % 2 == 0:
                        pe.wait_ge(fused_done, b * IT + (IT - 1 + k // 2))
                    transpose_rows(0, k, gu_bank[k // 2][k % 2])
                if isinstance(b, int) and b == 0:
                    pe.wait_ge(flaws_done, 1)
                down(b, NJ - 1, 1)

            ffn(0)
            with pe.Fori(1, NB - 1) as b:
                ffn(b)
            ffn_steps(NB - 1, NJ - 1)
            gate_up(NB - 1, NJ - 1, 0, NB * IT - 3)
            gate_up(NB - 1, NJ - 1, 1, NB * IT - 2)
            down(NB - 1, NJ - 2, 1)
            pe.wait_ge(f_lo_done, NB * IT - 1)
            down_rows(0, NJ - 1, 0, f_hi[:, 0, :], f_lo[:, 0, :])
            down_rows(1, NJ - 1, 0, f_hi[:, 0, :], f_lo[:, 0, :])
            pe.wait_ge(f_lo_done, NB * IT)
            down_rows(0, NJ - 1, 1, last_hi, last_lo)
            down_rows(1, NJ - 1, 1, last_hi, last_lo)
            for l in range(2, LT):
                down_rows(l, NJ - 1, 0, f_hi[:, 0, :], f_lo[:, 0, :])
                down_rows(l, NJ - 1, 1, last_hi, last_lo)


_INPUTS = {
    "x": "x", "ctx_tokens": "ctx_1024", "wq": "L0_xattn_Wq", "bq": "L0_xattn_bq", "wk": "L0_xattn_Wk",
    "bk": "L0_xattn_bk", "gate_w": "L0_ffn_gate_w", "up_w": "L0_ffn_up_w", "down_w": "L0_ffn_down_w",
    "gate_scale": "L0_ffn_gate_scale", "up_scale": "L0_ffn_up_scale", "down_scale": "L0_ffn_down_scale",
}


def kernel(**inputs):
    import numpy as np
    import concourse.bacc as bacc
    from concourse.bass_utils import run_bass_kernel_spmd

    nc = bacc.Bacc("TRN2", target_bir_lowering=False, num_devices=1)
    arrays, aps = {}, {}
    for name, key in _INPUTS.items():
        a = np.ascontiguousarray(inputs[key])
        arrays[f"in_{name}"] = a
        aps[name] = nc.dram_tensor(f"in_{name}", a.shape, mybir.dt.from_np(a.dtype), kind="ExternalInput").ap()
    out = nc.dram_tensor("out_x", arrays["in_x"].shape, F32, kind="ExternalOutput").ap()
    build_xattn_ffn(nc, out=out, **aps)
    result = run_bass_kernel_spmd(nc, [arrays], core_ids=[0])
    return result.results[0]["out_x"]
```
